# Optimizing a Trainium2 kernel written in Bass

```python
import numpy as np
import jax
import jax.numpy as jnp

def _softmax(x, axis=-1):
    return jax.nn.softmax(x, axis=axis)

def _gelu(x):
    return jax.nn.gelu(x, approximate=True)

def _silu(x):
    return jax.nn.silu(x)

def _sigmoid(x):
    return jax.nn.sigmoid(x)

def _layernorm(x, axis=-1, eps=1e-05):
    m = jnp.mean(x, axis=axis, keepdims=True)
    v = jnp.var(x, axis=axis, keepdims=True)
    return (x - m) / jnp.sqrt(v + eps)

def _scatter_add(tgt, idx, src, axis=0):
    return tgt.at[idx].add(src)

def _segment_sum(src, seg, n):
    return jax.ops.segment_sum(src, seg, n)
kernel_name = 'mk_cond_resid_d2_seqx_r4_30f280'

def setup_inputs(seed: int=0):
    np.random.seed(seed)
    _w = jnp.asarray

    def _rec_inputs():
        import jax
        import jax.numpy as jnp
        _rk = jax.random.key(seed)
        x = -0.000125 + 0.9999 * jax.random.normal(jax.random.fold_in(_rk, 1), (128, 64, 256), jnp.float32)
        _lenS = 64 - jax.random.randint(jax.random.fold_in(_rk, 7), (128,), 0, max(1, 64 // 4) + 1, jnp.int32)
        _lenS2 = 64 - jax.random.randint(jax.random.fold_in(_rk, 8), (128,), 0, max(1, 64 // 4) + 1, jnp.int32)
        cond_1024 = -0.00493535 + 1.00056 * jax.random.normal(jax.random.fold_in(_rk, 11), (128, 256), jnp.float32)
        return (x, cond_1024)
    x, cond_1024 = _rec_inputs()

    def _L0_cond_setup():
        import jax, jax.numpy as jnp
        import numpy as np
        INPUT_DIM = 256
        LATENT_DIM = 256
        key = jax.random.key(seed)
        ks = jax.random.split(key, 8)
        B, T = (64, 128)
        concat_dim = INPUT_DIM + LATENT_DIM
        s = lambda fan_in: 1.0 / np.sqrt(fan_in)
        return {'x': jax.random.normal(ks[0], (B, T, INPUT_DIM), dtype=jnp.float32), 'h0': jax.random.normal(ks[1], (B, LATENT_DIM), dtype=jnp.float32), 'w_W': jax.random.uniform(ks[2], (concat_dim, 2 * LATENT_DIM), jnp.float32, -s(concat_dim), s(concat_dim)), 'w_b': jax.random.uniform(ks[3], (2 * LATENT_DIM,), jnp.float32, -s(concat_dim), s(concat_dim)), 'wx_W': jax.random.uniform(ks[4], (INPUT_DIM, LATENT_DIM), jnp.float32, -s(INPUT_DIM), s(INPUT_DIM)), 'wx_b': jax.random.uniform(ks[5], (LATENT_DIM,), jnp.float32, -s(INPUT_DIM), s(INPUT_DIM)), 'wh_W': jax.random.uniform(ks[6], (LATENT_DIM, LATENT_DIM), jnp.float32, -s(LATENT_DIM), s(LATENT_DIM)), 'wh_b': jax.random.uniform(ks[7], (LATENT_DIM,), jnp.float32, -s(LATENT_DIM), s(LATENT_DIM))}
    _L0_cond_all = _L0_cond_setup()
    _L0_cond_in = {k: v for k, v in _L0_cond_all.items() if k in ('w_W', 'w_b', 'wx_W', 'wx_b', 'wh_W', 'wh_b')}
    del _L0_cond_all

    def _L1_cond_setup():
        import jax, jax.numpy as jnp
        import numpy as np
        D_MODEL = 256
        D_FF = 1024
        N_EXPERTS = 8
        TOP_K = 2
        N_SHARED = 2
        B, T = (4, 512)
        key = jax.random.key(seed)
        ks = jax.random.split(key, 9)
        Hs = D_FF // 2
        Hr = D_FF // 4
        inp = {'x': jax.random.normal(ks[0], (B, T, D_MODEL), dtype=jnp.float32), 't_emb': jax.random.normal(ks[1], (B, D_MODEL), dtype=jnp.float32), 'W_router': 0.01 * jax.random.normal(ks[2], (N_EXPERTS, 2 * D_MODEL), dtype=jnp.float32), 'router_bias': jnp.zeros((N_EXPERTS,), dtype=jnp.float32), 's_w1': 0.02 * jax.random.normal(ks[3], (N_SHARED, Hs, D_MODEL), dtype=jnp.float32), 's_w3': 0.02 * jax.random.normal(ks[4], (N_SHARED, Hs, D_MODEL), dtype=jnp.float32), 's_w2': 0.02 * jax.random.normal(ks[5], (N_SHARED, D_MODEL, Hs), dtype=jnp.float32), 'r_w1': 0.02 * jax.random.normal(ks[6], (N_EXPERTS, Hr, D_MODEL), dtype=jnp.float32), 'r_w2': 0.02 * jax.random.normal(ks[7], (N_EXPERTS, D_MODEL, Hr), dtype=jnp.float32)}
        return inp
    _L1_cond_all = _L1_cond_setup()
    _L1_cond_in = {k: v for k, v in _L1_cond_all.items() if k in ('W_router', 'router_bias', 's_w1', 's_w3', 's_w2', 'r_w1', 'r_w2')}
    del _L1_cond_all
    return {'x': x, 'cond_1024': cond_1024, 'L0_cond_w_W': _L0_cond_in['w_W'], 'L0_cond_w_b': _L0_cond_in['w_b'], 'L0_cond_wx_W': _L0_cond_in['wx_W'], 'L0_cond_wx_b': _L0_cond_in['wx_b'], 'L0_cond_wh_W': _L0_cond_in['wh_W'], 'L0_cond_wh_b': _L0_cond_in['wh_b'], 'L1_cond_W_router': _L1_cond_in['W_router'], 'L1_cond_router_bias': _L1_cond_in['router_bias'], 'L1_cond_s_w1': _L1_cond_in['s_w1'], 'L1_cond_s_w3': _L1_cond_in['s_w3'], 'L1_cond_s_w2': _L1_cond_in['s_w2'], 'L1_cond_r_w1': _L1_cond_in['r_w1'], 'L1_cond_r_w2': _L1_cond_in['r_w2']}

def reference(x, cond_1024, L0_cond_w_W, L0_cond_w_b, L0_cond_wx_W, L0_cond_wx_b, L0_cond_wh_W, L0_cond_wh_b, L1_cond_W_router, L1_cond_router_bias, L1_cond_s_w1, L1_cond_s_w3, L1_cond_s_w2, L1_cond_r_w1, L1_cond_r_w2):
    import jax
    import jax.numpy as jnp

    def _L0_cond_ref(x, h0, w_W, w_b, wx_W, wx_b, wh_W, wh_b):
        import jax, jax.numpy as jnp
        import numpy as np
        INPUT_DIM = 256
        LATENT_DIM = 256
        xT = jnp.swapaxes(x, 0, 1)

        def step(h, x_t):
            fused = jax.nn.sigmoid(jnp.concatenate([x_t, h], axis=-1) @ w_W + w_b)
            hidden_state, output_state = jnp.split(fused, 2, axis=-1)
            memory_state = x_t @ wx_W + wx_b + hidden_state * (h @ wh_W + wh_b)
            h_new = output_state * h + (1.0 - output_state) * jnp.tanh(memory_state)
            return (h_new, h_new)
        _, hs = jax.lax.scan(step, h0, xT)
        return jnp.swapaxes(hs, 0, 1)

    def _L1_cond_ref(x, t_emb, W_router, router_bias, s_w1, s_w3, s_w2, r_w1, r_w2):
        import jax, jax.numpy as jnp
        import numpy as np
        D_MODEL = 256
        D_FF = 1024
        N_EXPERTS = 8
        TOP_K = 2
        N_SHARED = 2
        B, T = (4, 512)
        Bn, Tn, C = x.shape
        N = Bn * Tn
        x_flat = x.reshape(N, C)
        t_flat = jnp.broadcast_to(t_emb[:, None, :], (Bn, Tn, C)).reshape(N, C)
        shared_out = jnp.zeros_like(x_flat)
        for e in range(N_SHARED):
            h = jax.nn.silu(x_flat @ s_w1[e].T) * (x_flat @ s_w3[e].T)
            shared_out = shared_out + h @ s_w2[e].T
        shared_out = shared_out / N_SHARED
        router_in = jnp.concatenate([x_flat, t_flat], axis=-1)
        s = jax.nn.sigmoid((router_in @ W_router.T).astype(jnp.float32))
        sel_scores = s + router_bias
        _, topk_idx = jax.lax.top_k(sel_scores, TOP_K)
        s_sel = jnp.take_along_axis(s, topk_idx, axis=1)
        denom = jnp.sum(s_sel, axis=1, keepdims=True)
        gates = jnp.where(denom > 1e-09, s_sel / (denom + 1e-09), 1.0 / TOP_K).astype(x.dtype)
        gates_full = jnp.sum(jax.nn.one_hot(topk_idx, N_EXPERTS, dtype=x.dtype) * gates[..., None], axis=1)
        routed_out = jnp.zeros_like(x_flat)
        for e in range(N_EXPERTS):
            h = jax.nn.gelu(x_flat @ r_w1[e].T, approximate=False)
            routed_out = routed_out + h @ r_w2[e].T * gates_full[:, e:e + 1]
        out = (shared_out + routed_out) / (N_SHARED + TOP_K)
        return out.reshape(Bn, Tn, C)
    x = x + _L0_cond_ref(x, cond_1024, L0_cond_w_W, L0_cond_w_b, L0_cond_wx_W, L0_cond_wx_b, L0_cond_wh_W, L0_cond_wh_b)
    x = x + _L1_cond_ref(x, cond_1024, L1_cond_W_router, L1_cond_router_bias, L1_cond_s_w1, L1_cond_s_w3, L1_cond_s_w2, L1_cond_r_w1, L1_cond_r_w2)
    return x

_drawn_inputs = setup_inputs


def setup_inputs(seed=0):
    import zlib

    import numpy as np

    out = dict(_drawn_inputs(seed))
    spreads = {'L1_cond_router_bias': (0.0, 0.727)}
    factors = {'L0_cond_w_b': 8.0,
     'L0_cond_wh_b': 3.864,
     'L1_cond_W_router': 8.0,
     'L1_cond_s_w1': 8.0,
     'L1_cond_s_w3': 8.0,
     'L1_cond_s_w2': 8.0,
     'L1_cond_r_w1': 5.917,
     'L1_cond_r_w2': 5.741}
    for name, (base, spread) in spreads.items():
        noise = np.random.default_rng([zlib.crc32(name.encode()), seed]).standard_normal(out[name].shape)
        drawn = base * np.exp(spread * noise) if base else spread * noise
        out[name] = jnp.asarray(drawn.astype(out[name].dtype))
    for name, factor in factors.items():
        out[name] = (out[name] * factor).astype(out[name].dtype)
    return out
```

```python
import concourse.bass as bass
from concourse import mybir
from contextlib import ExitStack

F32 = mybir.dt.float32
F32R = mybir.dt.float32r
U32 = mybir.dt.uint32
ACT = mybir.ActivationFunctionType
ALU = mybir.AluOpType
AX = mybir.AxisListType

P = 128
B, T, C = 128, 64, 256
KC = C // P
S = 4
N = S * B
G = T // S
E_SH, F_SH = 2, 512
E_RT, F_RT = 8, 256
U_SH = E_SH * F_SH // P
U_RT = E_RT * F_RT // P
UPE = F_RT // P
U = U_SH + U_RT
SLOTS = U // S
LAG = 2
TILES_SH, TILES_RT = 3 * KC, 2 * KC
TILES = U_SH * TILES_SH + U_RT * TILES_RT
CHUNK = 8 * P
SCAN_CHUNKS = 3
CHUNKS = SCAN_CHUNKS + TILES * P // CHUNK
W_GATES, W_X, W_H = 0, 2 * KC * 2 * C, 2 * KC * 2 * C + KC * C
BIAS_GATES, BIAS_X, BIAS_H = 0, 2 * C, 3 * C
MATS = 2 * U_SH + U_RT
DENOM_MIN = 1e-9


def unit_base(u):
    tiles = u * TILES_SH if u < U_SH else U_SH * TILES_SH + (u - U_SH) * TILES_RT
    return SCAN_CHUNKS * CHUNK + tiles * P


def mat_of(u, which):
    return 2 * u + which if u < U_SH else U_SH + u


def build(nc, xT, condT, cond, wall, biases, wrT, rbias, outT):
    ctx = ExitStack()
    with ctx:
        def sb(name, shape, dt=F32):
            return ctx.enter_context(nc.sbuf_tensor(name, shape, dt))

        def sem(name):
            return ctx.enter_context(nc.semaphore(name))

        w_hi = sb("w_hi", [P, CHUNKS * CHUNK], F32R)
        w_lo = sb("w_lo", [P, CHUNKS * CHUNK], F32R)
        bias_row = sb("bias_row", [2, 4 * C], F32R)
        ones2 = sb("ones2", [2, P], F32R)
        row0 = sb("row0", [2, 1])
        row1 = sb("row1", [2, 1])
        ident = sb("ident", [P, P])
        sel_f = sb("sel_f", [2 * E_RT, E_RT])
        sel = sb("sel", [2 * E_RT, E_RT], F32R)
        xin = [sb(f"xin{i}", [P, KC, S, B]) for i in range(2)]
        x_hi = [sb(f"x_hi{i}", [P, KC, B], F32R) for i in range(2)]
        x_lo = [sb(f"x_lo{i}", [P, KC, B], F32R) for i in range(2)]
        x2 = [sb(f"x2_{i}", [P, KC, S, B]) for i in range(2)]
        x2_hi = [sb(f"x2_hi{i}", [P, KC, S, B], F32R) for i in range(2)]
        x2_lo = [sb(f"x2_lo{i}", [P, KC, S, B], F32R) for i in range(2)]
        work = sb("work", [P, 4, N])
        act_out = [work[:, i, :] for i in range(2)]
        prod = [work[:, 2 + i, :] for i in range(2)]
        stage = [work[:, 2 * i:2 * i + 2, :].rearrange("p a n -> p (a n)") for i in range(2)]
        prod_hi = [sb(f"prod_hi{i}", [P, N], F32R) for i in range(2)]
        prod_lo = [sb(f"prod_lo{i}", [P, N], F32R) for i in range(2)]
        h = sb("h", [B, C])
        tanh_g = sb("tanh_g", [B, 2 * C])
        mem = sb("mem", [B, C])
        cand = sb("cand", [B, C])
        diff = mem
        hT_hi = sb("hT_hi", [P, KC * B], F32R)
        hT_lo = sb("hT_lo", [P, KC * B], F32R)
        wr_sb = sb("wr_sb", [P, 2 * KC, E_RT])
        z_cond = sb("z_cond", [B, E_RT])
        r_bias = sb("r_bias", [B, E_RT])
        iota_i = sb("iota_i", [B, E_RT], mybir.dt.int32)
        iota8 = sb("iota8", [B, E_RT])
        z_r = sb("z_r", [B, S, E_RT])
        s_r = sb("s_r", [B, S, E_RT])
        sel_score = sb("sel_score", [B, S, E_RT])
        best = sb("best", [B, S, 8])
        best_i = sb("best_i", [B, S, 8], U32)
        best_f = sb("best_f", [B, S, 2])
        mask1 = sb("mask1", [B, S, E_RT])
        mask = sb("mask", [B, S, E_RT])
        gate = sb("gate", [B, S, E_RT])
        denom = sb("denom", [B, S])
        valid = sb("valid", [B, S])
        recip = sb("recip", [B, S])
        evenly = sb("evenly", [B, S])
        gate_parts = sb("gate_parts", [B, S, 2 * E_RT])
        gT = sb("gT", [2 * E_RT, N], F32R)

        def bank(name):
            return ctx.enter_context(nc.psum_tensor(name, [P, N], F32))

        ps_z, ps_w, ps_t = bank("ps_z"), bank("ps_w"), bank("ps_t")
        ps_o = [bank(f"ps_o{c}") for c in range(KC)]
        ring = [bank(f"ring{i}") for i in range(3)]
        HW, XW = slice(0, C), slice(C, 2 * C)
        ZR = slice(KC * B, KC * B + S * E_RT)

        ld_const = sem("ld_const")
        ld_w = [sem(f"ld_w{i}") for i in range(2)]
        ld_x = [sem(f"ld_x{i}") for i in range(2)]
        st_out = [sem(f"st_out{i}") for i in range(2)]
        pool_step = sem("pool_step")
        const_done = sem("const_done")
        sel_done = sem("sel_done")
        bias_step = sem("bias_step")
        bias_done = sem("bias_done")
        w_hi_done = sem("w_hi_done")
        w_lo_done = sem("w_lo_done")
        zc_ready = sem("zc_ready")
        zc_done = sem("zc_done")
        xhi_done = sem("xhi_done")
        xlo_done = sem("xlo_done")
        z_ready = sem("z_ready")
        hw_ready = sem("hw_ready")
        tanh_done = sem("tanh_done")
        v_done = sem("v_done")
        mem_done = sem("mem_done")
        cand_done = sem("cand_done")
        diff_done = sem("diff_done")
        share_done = sem("share_done")
        h_done = sem("h_done")
        hT_ready = sem("hT_ready")
        hT_hi_done = sem("hT_hi_done")
        hT_lo_done = sem("hT_lo_done")
        x2_done = sem("x2_done")
        x2_hi_done = sem("x2_hi_done")
        x2_lo_done = sem("x2_lo_done")
        zr_ready = sem("zr_ready")
        zr_done = sem("zr_done")
        sig_done = sem("sig_done")
        router_step = sem("router_step")
        router_go = sem("router_go")
        router_valid = sem("router_valid")
        router_scaled = sem("router_scaled")
        gate_hi_done = sem("gate_hi_done")
        gates_done = sem("gates_done")
        gT_ready = sem("gT_ready")
        gT_done = sem("gT_done")
        l1_ready = sem("l1_ready")
        bc_ready = sem("bc_ready")
        act_done = sem("act_done")
        prod_done = sem("prod_done")
        hi_done = sem("hi_done")
        lo_done = sem("lo_done")
        l2_ready = sem("l2_ready")
        out_done = sem("out_done")

        def wait(eng, s, value):
            if not (isinstance(value, int) and value <= 0):
                eng.wait_ge(s, value)

        ROUTER_STEPS = 9 + 2 * S

        block = ctx.enter_context(nc.Block())

        def loop_groups(eng, body):
            body(0, 0, 0, True)
            with eng.Fori(0, (G - 4) // 2) as j:
                body(2 * j + 1, j, 1, True)
                body(2 * j + 2, j + 1, 0, True)
            for g in range(G - 3, G):
                body(g, g // 2, g % 2, g < G - 1)

        @block.sync
        def _(sp):
            sp.dma_start(xin[1][0:1, :, :, :].rearrange("p k s b -> p (k s b)"), biases).then_inc(ld_const, 16)
            sp.dma_start(xin[1][1:2, :, :, :].rearrange("p k s b -> p (k s b)"), biases).then_inc(ld_const, 16)
            sp.dma_start(x2[1][:, :, 0, :], condT).then_inc(ld_const, 16)
            sp.dma_start(h[:, :], cond).then_inc(ld_const, 16)
            sp.dma_start(wr_sb[:, :, :], wrT).then_inc(ld_const, 16)
            sp.dma_start(r_bias[:, :], rbias.partition_broadcast(B)).then_inc(ld_const, 16)
            for c in range(CHUNKS):
                if c >= 2:
                    sp.wait_ge(w_lo_done, c - 1)
                sp.dma_start(stage[c % 2], wall[c, :, :]).then_inc(ld_w[c % 2], 16)
                if c == 0:
                    sp.dma_start(xin[0][:, :, :, :], xT[0]).then_inc(ld_x[0], 16)
            sp.wait_ge(bias_done, 1)
            sp.dma_start(xin[1][:, :, :, :], xT[1]).then_inc(ld_x[1], 16)

            def body(g, half, par, scan):
                if scan:
                    wait(sp, x2_done, S * g + S)
                    if not (isinstance(g, int) and g + 2 >= G):
                        nxt = xT[g + 2] if isinstance(g, int) else xT[bass.ds(g + 2, 1)].rearrange("a p k s b -> (a p) k s b")
                        sp.dma_start(xin[par][:, :, :, :], nxt).then_inc(ld_x[par], 16)
                if not (isinstance(g, int) and g == 0):
                    wait(sp, out_done, KC * g)
                    prev = outT[g - 1] if isinstance(g, int) else outT[bass.ds(g - 1, 1)].rearrange("a p k s b -> (a p) k s b")
                    sp.dma_start(prev, x2[1 - par][:, :, :, :]).then_inc(st_out[1 - par], 16)

            loop_groups(sp, body)
            sp.wait_ge(out_done, KC * G)
            sp.dma_start(outT[G - 1], x2[(G - 1) % 2][:, :, :, :]).then_inc(st_out[(G - 1) % 2], 16)
            for par in range(2):
                sp.wait_ge(st_out[par], 16 * (G // 2))

        @block.tensor
        def _(pe):
            def three(out, w_col, n, x_hi_ap, x_lo_ap, start, stop):
                last = None
                for i, (w, x) in enumerate(((w_hi, x_hi_ap), (w_lo, x_hi_ap), (w_hi, x_lo_ap))):
                    last = pe.matmul(out, w[:, w_col:w_col + n], x, start=start and i == 0, stop=stop and i == 2)
                return last

            def three_state(out, hi, lo, w_col, n, start, stop):
                last = None
                for i, (a, w) in enumerate(((hi, w_hi), (hi, w_lo), (lo, w_hi))):
                    last = pe.matmul(out, a, w[:, w_col:w_col + n], start=start and i == 0, stop=stop and i == 2)
                return last

            def x_part(t, par):
                wait(pe, xlo_done, t + 1)
                wait(pe, tanh_done, t)
                wait(pe, mem_done, t)
                pe.matmul(ps_z[:, :], ones2[:, :], bias_row[:, BIAS_GATES:BIAS_GATES + 2 * C], start=True, stop=False)
                for k in range(KC):
                    three_state(ps_z[:, :], x_hi[par][:, k, :], x_lo[par][:, k, :], W_GATES + k * 2 * C, 2 * C, False, False)
                pe.matmul(ps_w[:, XW], ones2[:, :], bias_row[:, BIAS_X:BIAS_X + C], start=True, stop=False)
                for k in range(KC):
                    three_state(ps_w[:, XW], x_hi[par][:, k, :], x_lo[par][:, k, :], W_X + k * C, C, False, k == KC - 1)

            def h_part(t):
                wait(pe, hT_lo_done, t + 1)
                for k in range(KC):
                    hs = slice(k * B, (k + 1) * B)
                    last = three_state(ps_z[:, :], hT_hi[:, hs], hT_lo[:, hs], W_GATES + (KC + k) * 2 * C, 2 * C, False, k == KC - 1)
                last.then_inc(z_ready, 1)
                pe.matmul(ps_w[:, HW], ones2[:, :], bias_row[:, BIAS_H:BIAS_H + C], start=True, stop=False)
                for k in range(KC):
                    hs = slice(k * B, (k + 1) * B)
                    last = three_state(ps_w[:, HW], hT_hi[:, hs], hT_lo[:, hs], W_H + k * C, C, False, k == KC - 1)
                last.then_inc(hw_ready, 1)

            def transpose_state(t, g, s):
                wait(pe, h_done, t + 1)
                if s == 0:
                    wait(pe, gT_done, g + 1)
                for k in range(KC):
                    last = pe.transpose(ps_t[:, k * B:(k + 1) * B], h[:, k * P:(k + 1) * P], ident[:, :])
                last.then_inc(hT_ready, 1)

            def router(t, par, s):
                wait(pe, x2_done, t + 1)
                wait(pe, hT_lo_done, t + 2)
                for k in range(KC):
                    last = pe.matmul(ps_t[:, ZR.start + s * E_RT:ZR.start + (s + 1) * E_RT], x2[par][:, k, s, :],
                                     wr_sb[:, k, :], start=k == 0, stop=k == KC - 1)
                last.then_inc(zr_ready, 1)

            def transpose_gates(g):
                pe.wait_ge(gates_done, g + 1)
                for s in range(S):
                    last = pe.transpose(ps_t[0:2 * E_RT, s * B:(s + 1) * B], gate_parts[:, s, :], ident[:, :])
                last.then_inc(gT_ready, 1)

            def layer1(g, par, u):
                for which in range(2 if u < U_SH else 1):
                    m = mat_of(u, which)
                    if u < U_SH:
                        dst = ring[m % 3]
                        if m >= 3:
                            wait(pe, (act_done, prod_done)[(m - 3) % 2], U * g + (m - 3) // 2 + 1)
                        else:
                            wait(pe, (prod_done, act_done, act_done)[m], U * g - (0, 1, 0)[m])
                    else:
                        dst = ring[1 + (u - U_SH) % 2]
                        if u == U_SH:
                            wait(pe, prod_done, U * g + 7)
                        else:
                            wait(pe, act_done, U * g + (8 if u == U_SH + 1 else u - 1))
                    for k in range(KC):
                        last = three(dst[:, :], unit_base(u) + (which * KC + k) * P, P,
                                     x2_hi[par][:, k, :, :].rearrange("p s b -> p (s b)"),
                                     x2_lo[par][:, k, :, :].rearrange("p s b -> p (s b)"), k == 0, k == KC - 1)
                    last.then_inc(l1_ready, 1)

            def broadcast_gate(g, e):
                if e == 0:
                    pe.wait_ge(gT_done, g + 1)
                pe.wait_ge(prod_done, U * g + U_SH + UPE * e)
                pe.matmul(ring[0][:, :], sel[:, e:e + 1].to_broadcast([2 * E_RT, P]), gT[:, :], start=True, stop=True).then_inc(bc_ready, 1)

            def layer2(g, u):
                wait(pe, lo_done, U * g + u + 1)
                if u == 0:
                    wait(pe, out_done, KC * g)
                base = unit_base(u) + (2 if u < U_SH else 1) * KC * P
                for c in range(KC):
                    last = three(ps_o[c][:, :], base + c * P, P, prod_hi[u % 2][:, :], prod_lo[u % 2][:, :], u == 0, u == U - 1)
                last.then_inc(l2_ready, 1)

            pe.wait_ge(ld_const, 6 * 16)
            for k in range(KC):
                last = pe.matmul(ring[0][:, 0:E_RT], x2[1][:, k, 0, :], wr_sb[:, KC + k, :], start=k == 0, stop=k == KC - 1)
            last.then_inc(zc_ready, 1)
            pe.wait_ge(sel_done, 2)
            pe.wait_ge(const_done, 3)
            pe.wait_ge(bias_done, 1)
            pe.wait_ge(w_lo_done, SCAN_CHUNKS)
            for s in range(S):
                x_part(s, s % 2)
                h_part(s)
                transpose_state(s, -1, s)
                router(s, 0, s)
            pe.wait_ge(w_lo_done, CHUNKS)
            pe.wait_ge(zc_done, 1)

            def body(g, half, par, scan):
                wait(pe, x2_lo_done, S * g + S)
                for u in range(U):
                    layer1(g, par, u)
                    if u >= U_SH and (u - U_SH) % UPE == 0:
                        broadcast_gate(g, (u - U_SH) // UPE)
                    if u >= LAG:
                        layer2(g, u - LAG)
                    elif not (isinstance(g, int) and g == 0):
                        layer2(g - 1, U - LAG + u)
                    s, r = divmod(u, SLOTS)
                    t = S * g + (S + s)
                    if u == 3:
                        transpose_gates(g)
                    if scan and r == 0:
                        x_part(t, s % 2)
                    if scan and r == 1:
                        h_part(t)
                    if scan and r == 4:
                        transpose_state(t, g, s)
                    if scan and r == 5:
                        router(t, 1 - par, s)

            loop_groups(pe, body)
            layer2(G - 1, U - 2)
            layer2(G - 1, U - 1)

        @block.scalar
        def _(act):
            def weight_hi(c):
                act.wait_ge(ld_w[c % 2], 16 * (c // 2 + 1))
                act.activation(w_hi[:, c * CHUNK:(c + 1) * CHUNK], stage[c % 2], ACT.Copy).then_inc(w_hi_done, 1)

            def scan_gates(t):
                wait(act, z_ready, t + 1)
                wait(act, h_done, t)
                act.activation(tanh_g[:, :], ps_z[:, :], ACT.Tanh, scale=0.5).then_inc(tanh_done, 1)

            def scan_cand(t):
                wait(act, mem_done, t + 1)
                act.activation(cand[:, :], mem[:, :], ACT.Tanh).then_inc(cand_done, 1)

            chunk = SCAN_CHUNKS
            for c in range(SCAN_CHUNKS):
                weight_hi(c)
            for s in range(S):
                scan_gates(s)
                if chunk < CHUNKS:
                    weight_hi(chunk)
                    chunk += 1
                scan_cand(s)
                for _ in range(3):
                    if chunk < CHUNKS:
                        weight_hi(chunk)
                        chunk += 1

            def body(g, half, par, scan):
                for u in range(U):
                    s, r = divmod(u, SLOTS)
                    t = S * g + (S + s)
                    if scan and r == 2:
                        scan_gates(t)
                    if u == 0:
                        act.wait_ge(zr_done, g + 1)
                        act.activation(s_r[:, :, :], z_r[:, :, :], ACT.Sigmoid).then_inc(sig_done, 1)
                    wait(act, l1_ready, MATS * g + mat_of(u, 0) + 1)
                    wait(act, prod_done, U * g + u - 1)
                    src = ring[mat_of(u, 0) % 3] if u < U_SH else ring[1 + (u - U_SH) % 2]
                    act.activation(act_out[u % 2], src[:, :], ACT.Silu if u < U_SH else ACT.Gelu).then_inc(act_done, 1)
                    if scan and r == 2:
                        scan_cand(t)

            loop_groups(act, body)

        @block.vector
        def _(dve):
            def weight_lo(c):
                dve.wait_ge(w_hi_done, c + 1)
                cols = slice(c * CHUNK, (c + 1) * CHUNK)
                dve.tensor_tensor(w_lo[:, cols], stage[c % 2], w_hi[:, cols].bitcast(F32), ALU.subtract).then_inc(w_lo_done, 1)

            def split_x_hi(t, par_x, s):
                wait(dve, xlo_done, t - 1)
                wait(dve, hw_ready, t - 1)
                dve.tensor_copy(x_hi[s % 2][:, :, :], xin[par_x][:, :, s, :]).then_inc(xhi_done, 1)

            def scan_mem(t):
                wait(dve, tanh_done, t + 1)
                wait(dve, hw_ready, t + 1)
                wait(dve, cand_done, t)
                dve.scalar_tensor_tensor(mem[:, :], tanh_g[:, 0:C], 1.0, ps_w[:, HW], ALU.add, ALU.mult).then_inc(v_done, 1)
                wait(dve, v_done, t + 1)
                dve.scalar_tensor_tensor(mem[:, :], mem[:, :], 0.5, ps_w[:, XW], ALU.mult, ALU.add).then_inc(mem_done, 1)

            def scan_state(t):
                wait(dve, cand_done, t + 1)
                wait(dve, h_done, t)
                dve.tensor_tensor(diff[:, :], h[:, :], cand[:, :], ALU.subtract).then_inc(diff_done, 1)
                wait(dve, diff_done, t + 1)
                dve.scalar_tensor_tensor(diff[:, :], tanh_g[:, C:2 * C], 1.0, diff[:, :], ALU.add, ALU.mult).then_inc(share_done, 1)
                wait(dve, share_done, t + 1)
                wait(dve, hT_ready, t)
                dve.scalar_tensor_tensor(h[:, :], diff[:, :], 0.5, cand[:, :], ALU.mult, ALU.add).then_inc(h_done, 1)

            def state_out(t, par, s, store_wait):
                wait(dve, hT_ready, t + 1)
                wait(dve, hw_ready, t + 1)
                dve.tensor_copy(hT_hi[:, :], ps_t[:, 0:KC * B]).then_inc(hT_hi_done, 1)
                if store_wait is not None:
                    wait(dve, st_out[par], store_wait)
                dve.tensor_tensor(x2[par][:, :, s, :], ps_t[:, 0:KC * B].rearrange("p (k b) -> p k b", k=KC),
                                  xin[par][:, :, s, :], ALU.add).then_inc(x2_done, 1)
                wait(dve, hT_hi_done, t + 2)
                dve.tensor_tensor(hT_lo[:, :], ps_t[:, 0:KC * B], hT_hi[:, :].bitcast(F32), ALU.subtract).then_inc(hT_lo_done, 1)
                wait(dve, x2_done, t + 1)
                dve.tensor_copy(x2_hi[par][:, :, s, :], x2[par][:, :, s, :]).then_inc(x2_hi_done, 1)

            dve.memset(ones2[:, :].bitcast(F32), 1.0).then_inc(const_done, 1)
            dve.wait_ge(ld_const, 6 * 16)
            braw = xin[1][0:2, :, :, :].rearrange("p k s b -> p (k s b)")
            blo = x2[0][0:2, :, :, :].rearrange("p k s b -> p (k s b)")
            dve.tensor_copy(bias_row[:, :], braw).then_inc(bias_step, 1)
            dve.wait_ge(bias_step, 1)
            dve.tensor_tensor(blo, braw, bias_row[:, :].bitcast(F32), ALU.subtract).then_inc(bias_step, 1)
            dve.wait_ge(const_done, 3)
            dve.tensor_scalar(row1[:, :], row0[:, :], -1.0, 1.0, ALU.mult, ALU.add).then_inc(bias_step, 1)
            dve.wait_ge(bias_step, 3)
            dve.tensor_scalar(blo, blo, row1[:, :], None, ALU.mult).then_inc(bias_step, 1)
            dve.wait_ge(bias_step, 4)
            dve.scalar_tensor_tensor(bias_row[:, :], bias_row[:, :].bitcast(F32), row0[:, :], blo, ALU.mult, ALU.add).then_inc(bias_done, 1)
            dve.wait_ge(sel_done, 1)
            dve.tensor_copy(sel[:, :], sel_f[:, :]).then_inc(sel_done, 1)
            c_T = x2[1][:, :, 0, :]
            dve.tensor_copy(hT_hi[:, :].rearrange("p (k b) -> p k b", k=KC), c_T).then_inc(hT_hi_done, 1)
            dve.wait_ge(hT_hi_done, 1)
            dve.tensor_tensor(hT_lo[:, :].rearrange("p (k b) -> p k b", k=KC), c_T,
                              hT_hi[:, :].bitcast(F32).rearrange("p (k b) -> p k b", k=KC), ALU.subtract).then_inc(hT_lo_done, 1)
            dve.wait_ge(zc_ready, 1)
            dve.tensor_copy(z_cond[:, :], ring[0][:, 0:E_RT]).then_inc(zc_done, 1)
            dve.wait_ge(ld_x[0], 16)
            split_x_hi(0, 0, 0)
            chunk = SCAN_CHUNKS
            for c in range(SCAN_CHUNKS):
                weight_lo(c)
            for s in range(S):
                if s + 1 < S:
                    split_x_hi(s + 1, 0, s + 1)
                scan_mem(s)
                if chunk < CHUNKS:
                    weight_lo(chunk)
                    chunk += 1
                scan_state(s)
                if chunk < CHUNKS:
                    weight_lo(chunk)
                    chunk += 1
                state_out(s, 0, s, None)
                for _ in range(2):
                    if chunk < CHUNKS:
                        weight_lo(chunk)
                        chunk += 1
            dve.wait_ge(ld_x[1], 16)
            split_x_hi(S, 1, 0)

            def router_gates(g, first_half):
                step = [0 if first_half else 4 + 2 * S]

                def link(ins):
                    step[0] += 1
                    ins.then_inc(router_step, 1)
                    dve.wait_ge(router_step, ROUTER_STEPS * g + step[0])

                def over_experts(ap):
                    return ap.unsqueeze(2).to_broadcast([B, S, E_RT])

                if first_half:
                    dve.wait_ge(sig_done, g + 1)
                    link(dve.tensor_tensor(sel_score[:, :, :], s_r[:, :, :],
                                           r_bias[:, :].unsqueeze(1).to_broadcast([B, S, E_RT]), ALU.add))
                    dve.sem_inc(router_go, 1)
                    for s in range(S):
                        step[0] += 1
                        dve.max(best[:, s, :], sel_score[:, s, :]).then_inc(router_step, 1)
                    dve.wait_ge(router_step, ROUTER_STEPS * g + step[0])
                    dve.sem_inc(router_go, 1)
                    for s in range(S):
                        step[0] += 1
                        dve.max_index(best_i[:, s, :], best[:, s, :], sel_score[:, s, :]).then_inc(router_step, 1)
                    dve.wait_ge(router_step, ROUTER_STEPS * g + step[0])
                    link(dve.tensor_copy(best_f[:, :, :], best_i[:, :, 0:2]))
                    link(dve.tensor_tensor(mask1[:, :, :], iota8[:, :].unsqueeze(1).to_broadcast([B, S, E_RT]),
                                           best_f[:, :, 0:1].to_broadcast([B, S, E_RT]), ALU.is_equal))
                    link(dve.tensor_tensor(mask[:, :, :], iota8[:, :].unsqueeze(1).to_broadcast([B, S, E_RT]),
                                           best_f[:, :, 1:2].to_broadcast([B, S, E_RT]), ALU.is_equal))
                else:
                    link(dve.tensor_tensor(mask[:, :, :], mask[:, :, :], mask1[:, :, :], ALU.add))
                    link(dve.tensor_tensor(gate[:, :, :], mask[:, :, :], s_r[:, :, :], ALU.mult))
                    link(dve.tensor_reduce(denom[:, :], gate[:, :, :], AX.X, ALU.add))
                    dve.tensor_scalar(valid[:, :], denom[:, :], DENOM_MIN, None, ALU.is_gt).then_inc(router_valid, 1)
                    dve.tensor_scalar(denom[:, :], denom[:, :], DENOM_MIN, None, ALU.add).then_inc(router_valid, 1)
                    dve.wait_ge(router_valid, 4 * g + 2)
                    dve.reciprocal(recip[:, :], denom[:, :]).then_inc(router_valid, 1)
                    dve.tensor_scalar(evenly[:, :], valid[:, :], -1.0, 1.0, ALU.mult, ALU.add).then_inc(router_valid, 1)
                    dve.wait_ge(router_valid, 4 * g + 4)
                    link(dve.scalar_tensor_tensor(recip[:, :], recip[:, :], 2.0, valid[:, :], ALU.mult, ALU.mult))
                    dve.tensor_tensor(gate[:, :, :], gate[:, :, :], over_experts(recip[:, :]), ALU.mult).then_inc(router_scaled, 1)
                    dve.tensor_tensor(mask1[:, :, :], mask[:, :, :], over_experts(evenly[:, :]), ALU.mult).then_inc(router_scaled, 1)
                    dve.wait_ge(router_scaled, 2 * g + 2)
                    link(dve.tensor_tensor(gate[:, :, :], gate[:, :, :], mask1[:, :, :], ALU.add))
                    parts = gate_parts[:, :, :]
                    dve.tensor_copy(parts[:, :, 0:E_RT].bitcast(F32R), gate[:, :, :]).then_inc(gate_hi_done, 1)
                    dve.wait_ge(gate_hi_done, g + 1)
                    dve.tensor_tensor(parts[:, :, E_RT:2 * E_RT].bitcast(F32R), gate[:, :, :], parts[:, :, 0:E_RT], ALU.subtract)\
                        .then_inc(gates_done, 1)

            def body(g, half, par, scan):
                not_first = not (isinstance(g, int) and g == 0)
                for u in range(U):
                    s, r = divmod(u, SLOTS)
                    t = S * g + (S + s)
                    if u == 0:
                        dve.wait_ge(zr_ready, S * g + S)
                        dve.tensor_tensor(z_r[:, :, :], ps_t[:, ZR].rearrange("p (s e) -> p s e", s=S),
                                          z_cond[:, :].unsqueeze(1).to_broadcast([B, S, E_RT]), ALU.add).then_inc(zr_done, 1)
                    if u == 1:
                        router_gates(g, True)
                    if u == 2:
                        router_gates(g, False)
                    if u == 2 and not_first:
                        output(g - 1, 1 - par)
                    if u == 4:
                        dve.wait_ge(gT_ready, g + 1)
                        dve.tensor_copy(gT[:, :], ps_t[0:2 * E_RT, :]).then_inc(gT_done, 1)
                    if scan and r == 2:
                        scan_mem(t)
                        if s < S - 1:
                            split_x_hi(t + 1, 1 - par, s + 1)
                        elif not (isinstance(g, int) and g + 2 >= G):
                            wait(dve, ld_x[par], 16 * (half + 2))
                            split_x_hi(t + 1, par, 0)
                    if scan and r == 3:
                        scan_state(t)
                    if scan and r == 5:
                        state_out(t, 1 - par, s, 16 * (half + par) if s == 0 else None)
                    wait(dve, act_done, U * g + u + 1)
                    if u < U_SH:
                        factor = ring[mat_of(u, 1) % 3]
                        wait(dve, l1_ready, MATS * g + mat_of(u, 1) + 1)
                    else:
                        factor = ring[0]
                        wait(dve, bc_ready, E_RT * g + (u - U_SH) // UPE + 1)
                    wait(dve, lo_done, U * g + u - 1)
                    dve.tensor_tensor(prod[u % 2], act_out[u % 2], factor[:, :], ALU.mult).then_inc(prod_done, 1)
                    wait(dve, prod_done, U * g + u + 1)
                    wait(dve, l2_ready, U * g + u - 1)
                    dve.tensor_copy(prod_hi[u % 2][:, :], prod[u % 2]).then_inc(hi_done, 1)

            def output(g, par):
                wait(dve, l2_ready, U * g + U)
                for c in range(KC):
                    x2c = x2[par][:, c, :, :].rearrange("p s b -> p (s b)")
                    dve.scalar_tensor_tensor(x2c, ps_o[c][:, :], 1.0 / 8, x2c, ALU.mult, ALU.add).then_inc(out_done, 1)

            loop_groups(dve, body)
            output(G - 1, (G - 1) % 2)

        @block.gpsimd
        def _(pool):
            pool.memset(ident[:, :], 0.0).then_inc(pool_step, 1)
            pool.memset(row0[:, :], 0.0).then_inc(pool_step, 1)
            pool.memset(sel_f[:, :], 0.0).then_inc(pool_step, 1)
            pool.iota(iota_i[:, :], pattern=[[1, E_RT]], base=0, channel_multiplier=0).then_inc(pool_step, 1)
            pool.wait_ge(pool_step, 4)
            pool.affine_select(out=ident[:, :], in_=ident[:, :], compare_op=ALU.not_equal, fill=1.0, base=0,
                               pattern=[[-1, P]], channel_multiplier=1).then_inc(const_done, 1)
            pool.affine_select(out=row0[:, :], in_=row0[:, :], compare_op=ALU.not_equal, fill=1.0, base=0,
                               pattern=[[0, 1]], channel_multiplier=1).then_inc(const_done, 1)
            pool.affine_select(out=sel_f[:, :], in_=sel_f[:, :], compare_op=ALU.not_equal, fill=1.0, base=0,
                               pattern=[[-1, E_RT]], channel_multiplier=1).then_inc(pool_step, 1)
            pool.tensor_copy(iota8[:, :], iota_i[:, :]).then_inc(pool_step, 1)
            pool.wait_ge(pool_step, 6)
            pool.affine_select(out=sel_f[:, :], in_=sel_f[:, :], compare_op=ALU.not_equal, fill=1.0, base=-E_RT,
                               pattern=[[-1, E_RT]], channel_multiplier=1).then_inc(sel_done, 1)

            def split_x_lo(t, par_x, s):
                wait(pool, xhi_done, t + 1)
                pool.tensor_tensor(x_lo[s % 2][:, :, :], xin[par_x][:, :, s, :], x_hi[s % 2][:, :, :].bitcast(F32),
                                   ALU.subtract).then_inc(xlo_done, 1)

            def split_x2_lo(t, par, s):
                wait(pool, x2_hi_done, t + 1)
                pool.tensor_tensor(x2_lo[par][:, :, s, :], x2[par][:, :, s, :], x2_hi[par][:, :, s, :].bitcast(F32),
                                   ALU.subtract).then_inc(x2_lo_done, 1)

            split_x_lo(0, 0, 0)
            for s in range(S):
                if s + 1 < S:
                    split_x_lo(s + 1, 0, s + 1)
                split_x2_lo(s, 0, s)
            split_x_lo(S, 1, 0)

            def body(g, half, par, scan):
                for u in range(U):
                    s, r = divmod(u, SLOTS)
                    t = S * g + (S + s)
                    if scan and r == 2:
                        if s < S - 1:
                            split_x_lo(t + 1, 1 - par, s + 1)
                        elif not (isinstance(g, int) and g + 2 >= G):
                            split_x_lo(t + 1, par, 0)
                    if scan and r == 5:
                        split_x2_lo(t, 1 - par, s)
                    wait(pool, hi_done, U * g + u + 1)
                    pool.tensor_tensor(prod_lo[u % 2][:, :], prod[u % 2], prod_hi[u % 2][:, :].bitcast(F32),
                                       ALU.subtract).then_inc(lo_done, 1)

            loop_groups(pool, body)


_INS = ["xT", "condT", "cond", "wall", "biases", "wrT", "rbias"]


def _layout(i):
    import numpy as np
    a = {k: np.asarray(v) for k, v in i.items()}

    def tiles(w):
        return w.reshape(-1, P, w.shape[1]).transpose(1, 0, 2).reshape(P, -1)

    units = []
    for u in range(U_SH):
        e, f = divmod(u, F_SH // P)
        rows = slice(f * P, (f + 1) * P)
        units += [tiles(a["L1_cond_s_w1"][e, rows].T), tiles(a["L1_cond_s_w3"][e, rows].T), a["L1_cond_s_w2"][e][:, rows].T]
    for u in range(U_RT):
        e, f = divmod(u, UPE)
        rows = slice(f * P, (f + 1) * P)
        units += [tiles(a["L1_cond_r_w1"][e, rows].T), a["L1_cond_r_w2"][e][:, rows].T]
    wall = np.concatenate([tiles(a["L0_cond_w_W"]), tiles(a["L0_cond_wx_W"]), tiles(a["L0_cond_wh_W"])] + units, axis=1)
    return {
        "xT": a["x"].reshape(B, G, S, KC, P).transpose(1, 4, 3, 2, 0),
        "condT": a["cond_1024"].reshape(B, KC, P).transpose(2, 1, 0),
        "cond": a["cond_1024"],
        "wall": wall.reshape(P, CHUNKS, CHUNK).transpose(1, 0, 2),
        "biases": np.concatenate([a["L0_cond_w_b"], a["L0_cond_wx_b"], a["L0_cond_wh_b"]])[None],
        "wrT": a["L1_cond_W_router"].reshape(E_RT, 2 * KC, P).transpose(2, 1, 0),
        "rbias": a["L1_cond_router_bias"],
    }


def kernel(**inputs):
    import numpy as _np
    import concourse.bacc as _bacc
    from concourse import mybir as _mybir
    from concourse.bass_utils import run_bass_kernel_spmd as _run

    nc = _bacc.Bacc("TRN2", target_bir_lowering=False, num_devices=1)
    laid = _layout(inputs)
    arrays, args = {}, []
    for name in _INS:
        a = _np.ascontiguousarray(laid[name])
        arrays[f"in_{name}"] = a
        args.append(nc.dram_tensor(f"in_{name}", a.shape, _mybir.dt.from_np(a.dtype), kind="ExternalInput").ap())
    args.append(nc.dram_tensor("outT", (G, P, KC, S, B), _mybir.dt.float32, kind="ExternalOutput").ap())
    build(nc, *args)
    r = _run(nc, [arrays], core_ids=[0])
    out = r.results[0]["outT"]
    return _np.ascontiguousarray(out.transpose(4, 0, 3, 2, 1)).reshape(B, T, C)
```

```python
import concourse.bass as bass
from concourse import mybir
from contextlib import ExitStack

F32 = mybir.dt.float32
F32R = mybir.dt.float32r
U32 = mybir.dt.uint32
I32 = mybir.dt.int32
ACT = mybir.ActivationFunctionType
ALU = mybir.AluOpType
AX = mybir.AxisListType

P = 128
B, T, C = 128, 64, 256
KC = C // P
S = 4
N = S * B
G = T // S
TOKENS = B * T
K2 = 2
E_SH, F_SH = 2, 512
E_RT, F_RT = 8, 256
KF = F_RT // P
U = F_SH // P
LAG = 2
UNIT_COLS = 3 * KC * P
CHUNK = 1024
SCAN_CHUNKS = 3
SH_CHUNKS = U * UNIT_COLS // CHUNK
EARLY_CHUNKS = SCAN_CHUNKS + SH_CHUNKS
RT_BASE = EARLY_CHUNKS * CHUNK
SH_BASE = (SCAN_CHUNKS * CHUNK, RT_BASE + E_RT * CHUNK)
CHUNKS = EARLY_CHUNKS + E_RT + SH_CHUNKS
PIECE = 768
PIECES = EARLY_CHUNKS + G - 1


def piece(c):
    if isinstance(c, int) and c < EARLY_CHUNKS:
        return c * CHUNK, CHUNK
    first = EARLY_CHUNKS * CHUNK + (c - EARLY_CHUNKS) * PIECE
    return first, CHUNKS * CHUNK - first if isinstance(c, int) and c == PIECES - 1 else PIECE


W_GATES, W_X, W_H = 0, 2 * KC * 2 * C, 2 * KC * 2 * C + KC * C
DENOM_MIN = 1e-9

R = 2
TILE = R * P
TILES = K2 * TOKENS // TILE + E_RT
REGION = TOKENS + TILE
EMPTY = E_RT
ROWS_X = E_RT * REGION + E_RT * TILE


def build(nc, x, xT, condT, cond, wall, biases, wrT, rbias, out):
    rows_x = nc.dram_tensor("rows_x", [ROWS_X, C], F32, kind="Internal").ap()
    rows_y = nc.dram_tensor("rows_y", [TILES * TILE, C], F32, kind="Internal").ap()
    x2_d = nc.dram_tensor("x2_d", [G, B, S * C], F32, kind="Internal").ap()
    x2T_d = nc.dram_tensor("x2T_d", [G, P, KC * N], F32, kind="Internal").ap()
    part_d = nc.dram_tensor("part_d", [G, B, S * C], F32, kind="Internal").ap()
    ctx = ExitStack()
    with ctx:
        def sb(name, shape, dt=F32):
            return ctx.enter_context(nc.sbuf_tensor(name, shape, dt))

        def sem(name):
            return ctx.enter_context(nc.semaphore(name))

        w_hi = sb("w_hi", [P, CHUNKS * CHUNK], F32R)
        w_lo = sb("w_lo", [P, CHUNKS * CHUNK], F32R)
        row0 = sb("row0", [2, 1])
        row1 = sb("row1", [2, 1])
        ident = sb("ident", [P, P])
        before = sb("before", [P, P])
        ones = sb("ones", [P, P])

        buf = [sb(f"buf{i}", [P, S * C]) for i in range(8)]
        rbuf = [sb(f"rbuf{i}", [P, S * C], F32R) for i in range(4)]
        rhalf = [sb(f"rhalf{i}", [P, N], F32R) for i in range(4)]

        xin = [buf[i][:, :].rearrange("p (k s b) -> p k s b", k=KC, s=S) for i in range(2)]
        x_row = [buf[2][:, i * 2 * C:(i + 1) * 2 * C].rearrange("b (s c) -> b s c", s=2) for i in range(2)]
        part = buf[3]
        x2_row = [buf[4 + i][:, :].rearrange("b (s c) -> b s c", s=S) for i in range(2)]
        stage = buf[6][:, :]
        first_stage = (buf[6], buf[3], buf[7], buf[5], buf[6], buf[3])
        act_1 = buf[7][:, 0:N]
        grp_hi, grp_lo = rbuf[0][:, :], rbuf[1][:, :]
        x_hi = rbuf[2][:, 0:C].rearrange("p (k b) -> p k b", k=KC)
        x_lo = rbuf[2][:, C:2 * C].rearrange("p (k b) -> p k b", k=KC)
        hT_hi = rbuf[2][:, 2 * C:3 * C]
        hT_lo = rbuf[2][:, 3 * C:4 * C]
        bias_gates = rbuf[3][0:2, 0:2 * C]
        bias_x, bias_h = rbuf[3][0:2, 2 * C:3 * C], rbuf[3][0:2, 3 * C:4 * C]
        prod1_hi, prod1_lo = rhalf[0][:, :], rhalf[1][:, :]
        ones2 = rhalf[2][0:2, 0:P]
        condT_sb = buf[4][:, 0:C]
        h = sb("h", [B, C])
        tanh_g = sb("tanh_g", [B, 2 * C])
        mem = sb("mem", [B, C])
        cand = sb("cand", [B, C])
        keep = sb("keep", [B, C])
        renew = sb("renew", [B, C])
        wr_sb = sb("wr_sb", [P, 2 * KC, E_RT])
        z_cond = sb("z_cond", [B, E_RT])
        r_bias = sb("r_bias", [B, E_RT])
        iota_i = sb("iota_i", [B, E_RT], I32)
        iota8 = sb("iota8", [B, E_RT])
        z_r = sb("z_r", [B, S, E_RT])
        s_r = sb("s_r", [B, S, E_RT])
        score = sb("score", [B, S, E_RT])
        best = sb("best", [B, S, 8])
        best_i = sb("best_i", [B, S, 8], U32)
        expert = sb("expert", [B, S, K2])
        mask = [sb(f"mask{k}", [B, S, E_RT]) for k in range(K2)]
        both = sb("both", [B, S, E_RT])
        seen = sb("seen", [B, S + 1, E_RT])
        pos = sb("pos", [B, S, E_RT])
        tmp = [sb(f"tmp{k}", [B, S, E_RT]) for k in range(K2)]
        place = sb("place", [B, S, K2])
        picked = sb("picked", [B, S, K2])
        denom = sb("denom", [B, S])
        valid = sb("valid", [B, S])
        recip = sb("recip", [B, S])
        evenly = sb("evenly", [B, S])
        idx_x = [sb(f"idx_x{i}", [B, S, K2], U32) for i in range(2)]
        expert_all = sb("expert_all", [B, T, K2])
        place_all = sb("place_all", [B, T, K2])
        gate_all = sb("gate_all", [B, T, K2])
        zeros = sb("zeros", [P, C])
        count = sb("count", [P, E_RT])
        count_i = sb("count_i", [P, E_RT], I32)
        pad_at = sb("pad_at", [1, E_RT], I32)
        region_of = sb("region_of", [P, E_RT])
        tiles_of = sb("tiles_of", [P, E_RT])
        tiles_to = sb("tiles_to", [P, E_RT])
        y_base = sb("y_base", [P, E_RT])
        skip_rows = sb("skip_rows", [P, E_RT])
        tile_x = cand[:, :].bitcast(I32)[0:1, 0:TILES]
        tile_w = keep[:, :].bitcast(I32)[0:1, 0:TILES]
        tile_i = mem[:, :].bitcast(I32)[0:1, 0:TILES]
        xt = [buf[i // 2][:, i % 2 * R * C:(i % 2 + 1) * R * C] for i in range(4)]
        yt = [buf[2 + i // 2][:, i % 2 * R * C:(i % 2 + 1) * R * C] for i in range(4)]
        hid = [buf[4][:, i * R * F_RT:(i + 1) * R * F_RT] for i in range(2)]
        xt_hi = [rbuf[0][:, i * R * C:(i + 1) * R * C] for i in range(2)]
        xt_lo = [rbuf[1][:, i * R * C:(i + 1) * R * C] for i in range(2)]
        hid_hi = [rbuf[2][:, i * R * F_RT:(i + 1) * R * F_RT] for i in range(2)]
        hid_lo = [rbuf[3][:, i * R * F_RT:(i + 1) * R * F_RT] for i in range(2)]
        y_at = buf[7][:, 2 * C:2 * C + T * K2].rearrange("b (t k) -> b t k", k=K2)
        y_off = buf[7][:, 3 * C:3 * C + T * K2].rearrange("b (t k) -> b t k", k=K2)
        tile_f = buf[6][0:1, 0:TILES]
        past = buf[6][0:1, 768:768 + TILES]
        acc_e = buf[6][0:1, 256:256 + TILES]
        acc_r = buf[6][0:1, 512:512 + TILES]
        res = [buf[i][:, :].rearrange("b (s c) -> b s c", s=S) for i in range(2)]
        got = [[buf[2 + 2 * i + k][:, :].rearrange("b (s c) -> b s c", s=S) for k in range(K2)] for i in range(2)]
        act_out = [buf[6][:, i * N:(i + 1) * N] for i in range(2)]
        x2_in = buf[7]
        x2_hi = [rbuf[0][:, :], rbuf[2][:, :]]
        x2_lo = [rbuf[1][:, :], rbuf[3][:, :]]
        prod_hi = [rhalf[i][:, :] for i in range(2)]
        prod_lo = [rhalf[2 + i][:, :] for i in range(2)]
        old = tanh_g[:, :].bitcast(U32)
        idx_y = old[:, 0:T * K2].rearrange("b (t k) -> b t k", k=K2)
        idx_y_cur = [old[:, (T + i * S) * K2:(T + i * S + S) * K2].rearrange("b (t k) -> b t k", k=K2) for i in range(2)]
        gate_cur = tanh_g[:, C:C + S * K2].rearrange("b (t k) -> b t k", k=K2)

        bank = [ctx.enter_context(nc.psum_tensor(f"bank{i}", [P, N], F32)) for i in range(8)]
        ps_z, ps_w, ps_t = bank[0], bank[1], bank[2]
        HW, XW = slice(0, C), slice(C, 2 * C)
        ZR = slice(KC * B, KC * B + S * E_RT)
        POS = slice(ZR.stop, ZR.stop + S * E_RT)
        ps_l1, ps_l2 = bank[4:6], bank[6:8]
        ps_c = bank[3]
        ps_xt, ps_h, ps_ht, ps_y = (bank[2 * i:2 * i + 2] for i in range(4))
        ring, ps_o = (bank[0], bank[1], bank[2], bank[5]), (bank[3:5], bank[6:8])

        ld_const = sem("ld_const")
        ld_w = [sem(f"ld_w{i}") for i in range(4)]
        st_x2T = sem("st_x2T")
        ld_part = sem("ld_part")
        sp_go = sem("sp_go")
        st_part = sem("st_part")
        ld_x = [sem(f"ld_x{i}") for i in range(2)]
        ld_row = [sem(f"ld_row{i}") for i in range(2)]
        st_x2 = [sem(f"st_x2{i}") for i in range(2)]
        scattered = [sem(f"scattered{i}") for i in range(2 * S)]
        pads = sem("pads")
        st_empty = sem("st_empty")
        ld_t = [sem(f"ld_t{i}") for i in range(4)]
        st_t = [sem(f"st_t{i}") for i in range(4)]
        ld_res = [sem(f"ld_res{i}") for i in range(2)]
        gathered = [sem(f"gathered{i}") for i in range(2)]
        st_out = [sem(f"st_out{i}") for i in range(2)]
        pool_step = sem("pool_step")
        const_done = sem("const_done")
        bias_step = sem("bias_step")
        bias_done = sem("bias_done")
        w_hi_done = sem("w_hi_done")
        w_lo_done = sem("w_lo_done")
        zc_ready = sem("zc_ready")
        zc_done = sem("zc_done")
        x_hi_done = sem("x_hi_done")
        x_lo_done = sem("x_lo_done")
        xpart_ready = sem("xpart_ready")
        z_ready = sem("z_ready")
        hw_ready = sem("hw_ready")
        tanh_done = sem("tanh_done")
        v_done = sem("v_done")
        mem_done = sem("mem_done")
        cand_done = sem("cand_done")
        keep_done = sem("keep_done")
        renew_done = sem("renew_done")
        h_done = sem("h_done")
        hT_ready = sem("hT_ready")
        hT_hi_done = sem("hT_hi_done")
        hT_lo_done = sem("hT_lo_done")
        x2T_done = sem("x2T_done")
        x2_row_done = sem("x2_row_done")
        zr_ready = sem("zr_ready")
        zr_done = sem("zr_done")
        sig_done = sem("sig_done")
        router_go = sem("router_go")
        pool_go = sem("pool_go")
        router_step = sem("router_step")
        masks_done = sem("masks_done")
        pos_ready = sem("pos_ready")
        pos_done = sem("pos_done")
        idx_done = sem("idx_done")
        grp_hi_done = sem("grp_hi_done")
        grp_lo_done = sem("grp_lo_done")
        part_done = sem("part_done")
        l1a_ready = sem("l1a_ready")
        act1_done = sem("act1_done")
        prod1_done = sem("prod1_done")
        hi1_done = sem("hi1_done")
        lo1_done = sem("lo1_done")
        l2a_ready = sem("l2a_ready")
        count_ready = sem("count_ready")
        table_step = sem("table_step")
        pad_done = sem("pad_done")
        zeros_done = sem("zeros_done")
        tile_i_done = sem("tile_i_done")
        table_done = sem("table_done")
        xt_ready = sem("xt_ready")
        xt_hi_done = sem("xt_hi_done")
        xt_lo_done = sem("xt_lo_done")
        hid_ready = sem("hid_ready")
        hid_done = sem("hid_done")
        ht_ready = sem("ht_ready")
        ht_hi_done = sem("ht_hi_done")
        ht_lo_done = sem("ht_lo_done")
        y_ready = sem("y_ready")
        y_done = sem("y_done")
        l1_ready = sem("l1_ready")
        act_done = sem("act_done")
        prod_done = sem("prod_done")
        hi_done = sem("hi_done")
        lo_done = sem("lo_done")
        l2_ready = sem("l2_ready")
        ld_x2T = sem("ld_x2T")
        x2_hi_done = sem("x2_hi_done")
        x2_lo_done = sem("x2_lo_done")
        y_idx_step = sem("y_idx_step")
        y_idx_done = sem("y_idx_done")
        idx_cur_done = sem("idx_cur_done")
        gate_cur_done = sem("gate_cur_done")
        out_step = sem("out_step")
        out_done = sem("out_done")

        def wait(eng, s, value):
            if not (isinstance(value, int) and value <= 0):
                eng.wait_ge(s, value)

        def is_static(g):
            return isinstance(g, int)

        ROUTER_STEPS = 1 + S + S + 1 + K2 + 1 + 1 + (S - 1) + 4 * K2 + 1 + 3 + 4

        block = ctx.enter_context(nc.Block())

        def groups(eng, body):
            body(0, 0, 0)
            body(1, 0, 1)
            with eng.Fori(1, G // 2 - 1) as j:
                body(2 * j, j, 0)
                body(2 * j + 1, j, 1)
            body(G - 2, G // 2 - 1, 0)
            body(G - 1, G // 2 - 1, 1)

        @block.sync
        def _(sp):
            sp.dma_start(buf[1][0:1, :], biases).then_inc(ld_const, 16)
            sp.dma_start(buf[1][1:2, :], biases).then_inc(ld_const, 16)
            sp.dma_start(condT_sb, condT).then_inc(ld_const, 16)
            sp.dma_start(h[:, :], cond).then_inc(ld_const, 16)
            sp.dma_start(wr_sb[:, :, :], wrT).then_inc(ld_const, 16)
            sp.dma_start(r_bias[:, :], rbias.partition_broadcast(B)).then_inc(ld_const, 16)
            sp.dma_start(buf[0][:, :], xT[0]).then_inc(ld_x[0], 16)
            for c in range(4):
                sp.dma_start(first_stage[c][:, :], wall[:, c * CHUNK:(c + 1) * CHUNK]).then_inc(ld_w[c], 16)
            for i in range(2):
                sp.dma_start(x_row[i].rearrange("b s c -> b (s c)"), x[:, i * 2 * C:(i + 1) * 2 * C]).then_inc(ld_row[i], 16)
            sp.wait_ge(bias_done, 2)
            sp.dma_start(buf[1][:, :], xT[1]).then_inc(ld_x[1], 16)
            for c in range(4, EARLY_CHUNKS):
                sp.wait_ge(w_lo_done, c - 3)
                sp.dma_start(first_stage[c][:, :], wall[:, c * CHUNK:(c + 1) * CHUNK]).then_inc(ld_w[c - 4], 16)
            sp.wait_ge(zeros_done, 1)
            sp.dma_start(rows_x[EMPTY * REGION:ROWS_X, :].rearrange("(p j) c -> p j c", p=P),
                         zeros[:, :].unsqueeze(1).to_broadcast([P, R * E_RT, C])).then_inc(st_empty, 16)

            def pick(ap, g):
                return ap[g] if is_static(g) else ap[bass.ds(g, 1)].rearrange("a p n -> (a p) n")

            def load_rows(g, i):
                at = (g * S + 2 * i) * C
                sp.dma_start(x_row[i].rearrange("b s c -> b (s c)"),
                             x[:, at:at + 2 * C] if is_static(g) else x[:, bass.ds(at, 2 * C)]).then_inc(ld_row[i], 16)

            def store_part(g):
                wait(sp, part_done, g + 1)
                sp.dma_start(pick(part_d, g), part[:, :]).then_inc(st_part, 16)

            def load_part(g, stored):
                wait(sp, st_part, 16 * g)
                sp.sem_inc(sp_go, 1)
                if is_static(g) and g == 0:
                    sp.wait_ge(w_lo_done, EARLY_CHUNKS)
                wait(sp, *stored)
                sp.dma_start(part[:, :], pick(x2_d, g)).then_inc(ld_part, 16)

            def scan_body(g, half, par):
                started = not (is_static(g) and g == 0)
                more = not (is_static(g) and g == G - 1)
                if started:
                    wait(sp, x2T_done, S * g)
                    sp.dma_start(pick(x2T_d, g - 1), buf[1 - par][:, :]).then_inc(st_x2T, 16)
                if more:
                    wait(sp, x2_row_done, S * g + 2)
                    load_rows(g + 1, 0)
                if started and more:
                    wait(sp, st_x2T, 16 * g)
                    wait(sp, grp_lo_done, g)
                    wait(sp, zr_ready, S * g)
                    sp.dma_start(buf[1 - par][:, :], pick(xT, g + 1)).then_inc(ld_x[1 - par], 16)
                if not (is_static(g) and g < 2):
                    store_part(g - 2)
                if started:
                    load_part(g - 1, (st_x2[1 - par], 16 * (half + par)))
                if more:
                    wait(sp, w_lo_done, g + EARLY_CHUNKS if started else 5)
                    first, size = piece(g + EARLY_CHUNKS)
                    sp.dma_start(stage[:, 0:size], wall[:, first:first + size] if is_static(g) else wall[:, bass.ds(first, size)])                      .then_inc(ld_w[0], 16)
                wait(sp, x2_row_done, S * g + S)
                if more:
                    load_rows(g + 1, 1)
                sp.dma_start(pick(x2_d, g), buf[4 + par][:, :]).then_inc(st_x2[par], 16)

            groups(sp, scan_body)
            sp.wait_ge(x2T_done, T)
            sp.dma_start(x2T_d[G - 1], buf[1][:, :]).then_inc(st_x2T, 16)
            store_part(G - 2)
            load_part(G - 1, (st_x2[1], 16 * G // 2))

            sp.wait_ge(pad_done, 1)
            for e in range(E_RT):
                row = sp.value_load(pad_at[0:1, e:e + 1], min_val=e * REGION, max_val=e * REGION + TOKENS)
                sp.dma_start(rows_x[bass.ds(row, TILE), :].rearrange("(p r) c -> p r c", r=R),
                             zeros[:, :].unsqueeze(1).to_broadcast([P, R, C])).then_inc(pads, 16)
            sp.wait_ge(st_empty, 16)
            sp.wait_ge(st_x2T, 16 * G)
            sp.wait_ge(grp_lo_done, G)
            sp.wait_ge(zr_ready, T)
            sp.wait_ge(table_done, 1)
            for i in range(2 * S):
                sp.wait_ge(scattered[i], 16 * K2 * G // 2)
            sp.wait_ge(pads, 16 * E_RT)

            def load_tile(i, jj, q):
                wait(sp, xt_ready, i - 3)
                row = sp.value_load(tile_x[0:1, bass.ds(i, 1)], min_val=0, max_val=ROWS_X - TILE)
                sp.dma_start(xt[q], rows_x[bass.ds(row, TILE), :].rearrange("(p r) c -> p (r c)", r=R)).then_inc(ld_t[q], 16)

            def store_tile(i, q):
                wait(sp, y_done, i + 1)
                dst = rows_y[i * TILE:(i + 1) * TILE, :] if is_static(i) else rows_y[bass.ds(i * TILE, TILE), :]
                sp.dma_start(dst.rearrange("(p r) c -> p (r c)", r=R), yt[q]).then_inc(st_t[q], 16)

            BEHIND = 7
            for i in range(8):
                load_tile(i, i // 4, i % 4)
                if i == 3:
                    store_part(G - 1)
                    sp.wait_ge(y_idx_done, 1)
                    sp.dma_start(x2_in[:, :], x2T_d[0]).then_inc(ld_x2T, 16)
                if i >= BEHIND:
                    store_tile(i - BEHIND, (i - BEHIND) % 4)
            with sp.Fori(2, TILES // 4) as jj:
                for q in range(4):
                    load_tile(4 * jj + q, jj, q)
                    store_tile(4 * jj + (q - BEHIND), (q - BEHIND) % 4)
            for i in range(TILES, TILES + BEHIND):
                store_tile(i - BEHIND, (i - BEHIND) % 4)

            sp.wait_ge(st_part, 16 * G)
            sp.wait_ge(xt_ready, TILES)

            def store_out(g, par):
                wait(sp, out_done, g + 1)
                dst = out[:, g * S * C:(g + 1) * S * C] if is_static(g) else out[:, bass.ds(g * (S * C), S * C)]
                sp.dma_start(dst, buf[par][:, :]).then_inc(st_out[par], 16)

            def shared_body(g, half, par):
                if not (is_static(g) and g == G - 1):
                    wait(sp, x2_lo_done, g + 1)
                    sp.dma_start(x2_in[:, :], pick(x2T_d, g + 1)).then_inc(ld_x2T, 16)
                if not (is_static(g) and g < 2):
                    store_out(g - 2, par)
                    wait(sp, st_out[par], 16 * half)
                sp.dma_start(buf[par][:, :], pick(part_d, g)).then_inc(ld_res[par], 16)

            groups(sp, shared_body)
            store_out(G - 2, 0)
            store_out(G - 1, 1)
            for par in range(2):
                sp.wait_ge(st_out[par], 16 * G // 2)

        @block.tensor
        def _(pe):
            def three_state(out, hi, lo, w_col, n, start, stop):
                last = None
                for i, (a, w) in enumerate(((hi, w_hi), (hi, w_lo), (lo, w_hi))):
                    cols = slice(w_col, w_col + n) if is_static(w_col) else bass.ds(w_col, n)
                    last = pe.matmul(out, a, w[:, cols], start=start and i == 0, stop=stop and i == 2)
                return last

            def x_part(t):
                wait(pe, x_lo_done, t + 1)
                wait(pe, tanh_done, t)
                pe.matmul(ps_z[:, :], ones2, bias_gates, start=True, stop=False)
                for k in range(KC):
                    three_state(ps_z[:, :], x_hi[:, k, :], x_lo[:, k, :], W_GATES + k * 2 * C, 2 * C, False, False)
                wait(pe, mem_done, t)
                pe.matmul(ps_w[:, XW], ones2, bias_x, start=True, stop=False)
                for k in range(KC):
                    last = three_state(ps_w[:, XW], x_hi[:, k, :], x_lo[:, k, :], W_X + k * C, C, False, k == KC - 1)
                last.then_inc(xpart_ready, 1)

            def h_part(t):
                wait(pe, hT_hi_done, t + 1)
                for k in range(KC):
                    hs = slice(k * B, (k + 1) * B)
                    w = slice(W_GATES + (KC + k) * 2 * C, W_GATES + (KC + k + 1) * 2 * C)
                    pe.matmul(ps_z[:, :], hT_hi[:, hs], w_hi[:, w], start=False, stop=False)
                    pe.matmul(ps_z[:, :], hT_hi[:, hs], w_lo[:, w], start=False, stop=False)
                wait(pe, hT_lo_done, t + 1)
                for k in range(KC):
                    hs = slice(k * B, (k + 1) * B)
                    w = slice(W_GATES + (KC + k) * 2 * C, W_GATES + (KC + k + 1) * 2 * C)
                    last = pe.matmul(ps_z[:, :], hT_lo[:, hs], w_hi[:, w], start=False, stop=k == KC - 1)
                last.then_inc(z_ready, 1)
                pe.matmul(ps_w[:, HW], ones2, bias_h, start=True, stop=False)
                for k in range(KC):
                    hs = slice(k * B, (k + 1) * B)
                    last = three_state(ps_w[:, HW], hT_hi[:, hs], hT_lo[:, hs], W_H + k * C, C, False, k == KC - 1)
                last.then_inc(hw_ready, 1)

            def router(t, par_x, s):
                wait(pe, x2T_done, t + 1)
                for k in range(KC):
                    last = pe.matmul(ps_t[:, ZR.start + s * E_RT:ZR.start + (s + 1) * E_RT], xin[par_x][:, k, s, :],
                                     wr_sb[:, k, :], start=k == 0, stop=k == KC - 1)
                last.then_inc(zr_ready, 1)

            def layer1(dst, base, hi, lo):
                for k in range(KC):
                    for i, (w, xx) in enumerate(((w_hi, hi), (w_lo, hi), (w_hi, lo))):
                        last = pe.matmul(dst[:, :], w[:, base + k * P:base + (k + 1) * P], xx[:, k * N:(k + 1) * N],
                                         start=k == 0 and i == 0, stop=k == KC - 1 and i == 2)
                return last

            def layer2(dst, expert, u, hi, lo):
                col = SH_BASE[expert] + u * UNIT_COLS + 2 * KC * P
                for s in range(S):
                    hs = slice(s * B, (s + 1) * B)
                    half_bank = slice(s % 2 * C, (s % 2 + 1) * C)
                    for i, (a, w) in enumerate(((hi, w_hi), (hi, w_lo), (lo, w_hi))):
                        last = pe.matmul(dst[s // 2][:, half_bank], a[:, hs], w[:, col:col + C],
                                         start=u == 0 and s % 2 == 0 and i == 0, stop=u == U - 1 and i == 2,
                                         skip_group_check=True)
                return last

            def unit_layer1(g, u):
                n = U * g + u
                wait(pe, grp_lo_done, g + 1)
                for which, used in enumerate((act1_done, prod1_done)):
                    wait(pe, used, n)
                    layer1(ps_l1[which], SH_BASE[0] + u * UNIT_COLS + which * KC * P, grp_hi, grp_lo).then_inc(l1a_ready, 1)

            def unit_layer2(g, u):
                wait(pe, lo1_done, U * g + u + 1)
                if u == 0:
                    wait(pe, part_done, g)
                layer2(ps_l2, 0, u, prod1_hi, prod1_lo).then_inc(l2a_ready, 1)

            def places(g):
                wait(pe, masks_done, g + 1)
                pe.matmul(ps_t[:, POS], before[:, :], both[:, :, :].rearrange("b s e -> b (s e)"), start=True, stop=False)
                pe.matmul(ps_t[:, POS], ones[:, :], seen[:, 0:S, :].rearrange("b s e -> b (s e)"), start=False, stop=True)\
                  .then_inc(pos_ready, 1)

            def transpose_state(t):
                wait(pe, h_done, t + 1)
                wait(pe, x2T_done, t)
                for k in range(KC):
                    last = pe.transpose(ps_t[:, k * B:(k + 1) * B], h[:, k * P:(k + 1) * P], ident[:, :])
                last.then_inc(hT_ready, 1)

            pe.wait_ge(ld_const, 6 * 16)
            for k in range(KC):
                last = pe.matmul(ps_c[:, 0:E_RT], condT_sb[:, k * B:(k + 1) * B], wr_sb[:, KC + k, :], start=k == 0, stop=k == KC - 1)
            last.then_inc(zc_ready, 1)
            pe.wait_ge(const_done, 5)
            pe.wait_ge(bias_done, 2)
            pe.wait_ge(w_lo_done, SCAN_CHUNKS)
            x_part(0)

            def scan_body(g, half, par):
                for s in range(S):
                    t = S * g + s
                    h_part(t)
                    if not (is_static(g) and t == 0):
                        router(t - 1, par if s > 0 else 1 - par, (s - 1) % S)
                    if not (is_static(g) and t == T - 1):
                        x_part(t + 1)
                    if not (is_static(g) and g == 0):
                        if s == 0 and is_static(g) and g == 1:
                            pe.wait_ge(w_lo_done, EARLY_CHUNKS)
                        unit_layer1(g - 1, s)
                        if s == 2:
                            places(g - 1)
                    if s == 0:
                        wait(pe, zr_done, g)
                    if s == 3:
                        wait(pe, pos_done, g)
                    transpose_state(t)
                    if s > 0 and not (is_static(g) and g == 0):
                        unit_layer2(g - 1, s - 1)
                    if s == 0 and not (is_static(g) and g < 2):
                        unit_layer2(g - 2, U - 1)

            groups(pe, scan_body)
            router(T - 1, 1, S - 1)
            unit_layer2(G - 2, U - 1)
            unit_layer1(G - 1, 0)
            places(G - 1)
            pe.wait_ge(zc_done, 1)
            pe.matmul(ps_c[:, 0:E_RT], ones[:, :], seen[:, S, :], start=True, stop=True).then_inc(count_ready, 1)
            for u in range(1, U):
                unit_layer1(G - 1, u)
                unit_layer2(G - 1, u - 1)
            unit_layer2(G - 1, U - 1)

            pe.wait_ge(w_lo_done, PIECES)
            pe.wait_ge(table_done, 1)

            def weights_of(i):
                return pe.snap(pe.value_load(tile_w[0:1, bass.ds(i, 1)], min_val=RT_BASE, max_val=RT_BASE + (E_RT - 1) * CHUNK))

            def turn(out, rows):
                for k in range(KC):
                    for r in range(R):
                        last = pe.transpose(out[:, k * TILE + r * P:k * TILE + (r + 1) * P],
                                            rows[:, r * C + k * P:r * C + (k + 1) * P], ident[:, :])
                return last

            def product(out, hi, lo, col):
                for r in range(R):
                    for k in range(KC):
                        ks = slice(k * TILE + r * P, k * TILE + (r + 1) * P)
                        last = three_state(out[:, r * C:(r + 1) * C], hi[:, ks], lo[:, ks], col + k * C, C, k == 0, k == KC - 1)
                return last

            def turn_rows(i, q):
                wait(pe, xt_lo_done, i - 1)
                turn(ps_xt[q % 2], xt[q]).then_inc(xt_ready, 1)

            def first_layer(i, q, col):
                wait(pe, xt_lo_done, i + 1)
                wait(pe, hid_done, i - 1)
                product(ps_h[q % 2], xt_hi[q % 2], xt_lo[q % 2], col).then_inc(hid_ready, 1)

            def turn_hidden(i, q):
                wait(pe, hid_done, i + 1)
                wait(pe, ht_lo_done, i - 1)
                turn(ps_ht[q % 2], hid[q % 2]).then_inc(ht_ready, 1)

            def second_layer(i, q, col):
                wait(pe, ht_lo_done, i + 1)
                wait(pe, y_done, i - 1)
                product(ps_y[q % 2], hid_hi[q % 2], hid_lo[q % 2], col + KC * F_RT).then_inc(y_ready, 1)

            def slot(i, jj, q):
                first = not is_static(i) or 1 <= i <= TILES
                second = not is_static(i) or 3 <= i
                if first:
                    first_col = weights_of(i - 1)
                if not is_static(i) or i < TILES:
                    wait(pe, ld_t[q], 16 * (jj + 1))
                    turn_rows(i, q)
                if first:
                    first_layer(i - 1, (q - 1) % 4, first_col)
                if second:
                    second_col = weights_of(i - 3)
                if not is_static(i) or 2 <= i <= TILES + 1:
                    turn_hidden(i - 2, (q - 2) % 4)
                if second:
                    second_layer(i - 3, (q - 3) % 4, second_col)

            for i in range(4):
                slot(i, 0, i)
            with pe.Fori(1, TILES // 4) as jj:
                for q in range(4):
                    slot(4 * jj + q, jj, q)
            for i in range(TILES, TILES + 3):
                slot(i, 0, i % 4)

            def shared_body(g, half, par):
                wait(pe, x2_lo_done, g + 1)
                if is_static(g) and g == 1:
                    pe.wait_ge(y_done, TILES)
                for u in range(U):
                    n = U * g + u
                    for which, used in enumerate((act_done, prod_done)):
                        wait(pe, used, n - 1)
                        layer1(ring[2 * (u % 2) + which], SH_BASE[1] + u * UNIT_COLS + which * KC * P,
                               x2_hi[par], x2_lo[par]).then_inc(l1_ready, 1)
                    if not (is_static(g) and g == 0 and u < LAG):
                        wait(pe, lo_done, n - LAG + 1)
                        if u == LAG:
                            wait(pe, out_done, g - 1)
                        layer2(ps_o[par if u >= LAG else 1 - par], 1, (u - LAG) % U, prod_hi[u % 2], prod_lo[u % 2]).then_inc(l2_ready, 1)

            groups(pe, shared_body)
            for u in range(U - LAG, U):
                wait(pe, lo_done, U * (G - 1) + u + 1)
                layer2(ps_o[1], 1, u, prod_hi[u % 2], prod_lo[u % 2]).then_inc(l2_ready, 1)

        @block.scalar
        def _(act):
            def weight_hi(c):
                early = is_static(c) and c < EARLY_CHUNKS
                if early:
                    wait(act, ld_w[c % 4], 16 * (c // 4 + 1))
                else:
                    wait(act, ld_w[0], 16 * (c - EARLY_CHUNKS + 3))
                first, size = piece(c)
                dst = w_hi[:, first:first + size] if is_static(c) else w_hi[:, bass.ds(first, size)]
                act.activation(dst, first_stage[c][:, :] if early else stage[:, 0:size], ACT.Copy).then_inc(w_hi_done, 1)

            for c in range(SCAN_CHUNKS):
                weight_hi(c)

            def scores(g):
                wait(act, zr_done, g + 1)
                act.activation(s_r[:, :, :], z_r[:, :, :], ACT.Sigmoid).then_inc(sig_done, 1)

            def group_hi(g, par, last):
                wait(act, x2T_done, S * g + (S if last else S - 1))
                if not last:
                    wait(act, l1a_ready, 2 * U * g)
                steps = slice(S - 1, S) if last else slice(0, S - 1)
                act.activation(grp_hi.rearrange("p (k s b) -> p k s b", k=KC, s=S)[:, :, steps, :],
                               xin[par][:, :, steps, :], ACT.Copy).then_inc(grp_hi_done, 1)

            def unit_silu(g, u):
                n = U * g + u
                wait(act, l1a_ready, 2 * n + 1)
                wait(act, lo1_done, n)
                act.activation(act_1, ps_l1[0][:, :], ACT.Silu).then_inc(act1_done, 1)

            def unit_hi(g, u):
                n = U * g + u
                wait(act, prod1_done, n + 1)
                wait(act, l2a_ready, n)
                act.activation(prod1_hi, act_1, ACT.Copy).then_inc(hi1_done, 1)

            def scan_body(g, half, par):
                started = not (is_static(g) and g == 0)
                for s in range(S):
                    t = S * g + s
                    if s == 0 and started:
                        group_hi(g - 1, 1 - par, True)
                    wait(act, z_ready, t + 1)
                    wait(act, h_done, t)
                    act.activation(tanh_g[:, :], ps_z[:, :], ACT.Tanh, scale=0.5).then_inc(tanh_done, 1)
                    wait(act, mem_done, t + 1)
                    act.activation(cand[:, :], mem[:, :], ACT.Tanh).then_inc(cand_done, 1)
                    if s == 0 and started:
                        scores(g - 1)
                        weight_hi(g + EARLY_CHUNKS - 1)
                    if not started and s < SH_CHUNKS:
                        weight_hi(SCAN_CHUNKS + s)
                    if started:
                        unit_silu(g - 1, s)
                    if s == S - 1:
                        group_hi(g, par, False)
                    if started:
                        unit_hi(g - 1, s)

            groups(act, scan_body)
            group_hi(G - 1, 1, True)
            scores(G - 1)
            for u in range(U):
                unit_silu(G - 1, u)
                unit_hi(G - 1, u)

            def rows_hi(i, q):
                wait(act, xt_ready, i + 1)
                wait(act, hid_ready, i - 1)
                act.activation(xt_hi[q % 2], ps_xt[q % 2][:, :], ACT.Copy).then_inc(xt_hi_done, 1)

            def gelu(i, q):
                wait(act, hid_ready, i + 1)
                wait(act, ht_ready, i - 1)
                act.activation(hid[q % 2], ps_h[q % 2][:, :], ACT.Gelu).then_inc(hid_done, 1)

            def y_out(i, jj, q):
                wait(act, y_ready, i + 1)
                wait(act, st_t[q], 16 * jj)
                act.activation(yt[q], ps_y[q % 2][:, :], ACT.Copy).then_inc(y_done, 1)

            def slot(i, jj, q):
                if not is_static(i) or i < TILES:
                    rows_hi(i, q)
                if not is_static(i) or 1 <= i <= TILES:
                    gelu(i - 1, (q - 1) % 4)
                if not is_static(i) or 3 <= i:
                    y_out(i - 3, jj - (1 if q < 3 else 0), (q - 3) % 4)

            def x2_hi_of(g, par):
                wait(act, ld_x2T, 16 * (g + 1))
                wait(act, l1_ready, 2 * U * (g - 1))
                act.activation(x2_hi[par], x2_in[:, :], ACT.Copy).then_inc(x2_hi_done, 1)

            for i in range(8):
                if i == 3:
                    act.wait_ge(st_part, 16 * G)
                slot(i, i // 4, i % 4)
            with act.Fori(2, TILES // 4) as jj:
                for q in range(4):
                    slot(4 * jj + q, jj, q)
            slot(TILES, TILES // 4, 0)
            act.wait_ge(hid_ready, TILES)
            x2_hi_of(0, 0)
            for i in range(TILES + 1, TILES + 3):
                slot(i, TILES // 4, i % 4)

            def shared_body(g, half, par):
                for u in range(U):
                    n = U * g + u
                    wait(act, l1_ready, 2 * n + 1)
                    wait(act, lo_done, n - 1)
                    act.activation(act_out[u % 2], ring[2 * (u % 2)][:, :], ACT.Silu).then_inc(act_done, 1)
                    if u == 2 and not (is_static(g) and g == G - 1):
                        x2_hi_of(g + 1, 1 - par)
                    wait(act, prod_done, n + 1)
                    wait(act, l2_ready, n - 1)
                    act.activation(prod_hi[u % 2], act_out[u % 2], ACT.Copy).then_inc(hi_done, 1)

            groups(act, shared_body)

        @block.vector
        def _(dve):
            dve.memset(ones2.bitcast(F32), 1.0).then_inc(const_done, 1)
            dve.memset(seen[:, :, :], 0.0).then_inc(const_done, 1)
            dve.wait_ge(ld_const, 6 * 16)
            for i in range(2):
                cols = slice(i * 2 * C, (i + 1) * 2 * C)
                raw, rest, bias = buf[1][0:2, cols], buf[4][0:2, C:3 * C], rbuf[3][0:2, cols]
                dve.tensor_copy(bias, raw).then_inc(bias_step, 1)
                dve.wait_ge(bias_step, 4 * i + 1)
                dve.tensor_tensor(rest, raw, bias.bitcast(F32), ALU.subtract).then_inc(bias_step, 1)
                dve.wait_ge(const_done, 5)
                dve.tensor_scalar(row1[:, :], row0[:, :], -1.0, 1.0, ALU.mult, ALU.add).then_inc(bias_step, 1)
                dve.wait_ge(bias_step, 4 * i + 3)
                dve.tensor_scalar(rest, rest, row1[:, :], None, ALU.mult).then_inc(bias_step, 1)
                dve.wait_ge(bias_step, 4 * i + 4)
                dve.scalar_tensor_tensor(bias, bias.bitcast(F32), row0[:, :], rest, ALU.mult, ALU.add).then_inc(bias_done, 1)
            c_T = condT_sb
            dve.tensor_copy(hT_hi, c_T).then_inc(hT_hi_done, 1)
            dve.wait_ge(hT_hi_done, 1)
            dve.tensor_tensor(hT_lo, c_T, hT_hi.bitcast(F32), ALU.subtract).then_inc(hT_lo_done, 1)
            dve.wait_ge(zc_ready, 1)
            dve.tensor_copy(z_cond[:, :], ps_c[:, 0:E_RT]).then_inc(zc_done, 1)

            def split_x(t, half, par_x, s):
                if s == 0:
                    wait(dve, ld_x[par_x], 16 * (half + 1))
                wait(dve, xpart_ready, t)
                dve.tensor_copy(x_hi, xin[par_x][:, :, s, :]).then_inc(x_hi_done, 1)
                wait(dve, x_hi_done, t + 1)
                dve.tensor_tensor(x_lo, xin[par_x][:, :, s, :], x_hi.bitcast(F32), ALU.subtract).then_inc(x_lo_done, 1)

            def split_weight_lo(c):
                wait(dve, w_hi_done, c + 1)
                early = is_static(c) and c < EARLY_CHUNKS
                first, size = piece(c)
                cols = slice(first, first + size) if is_static(c) else bass.ds(first, size)
                dve.tensor_tensor(w_lo[:, cols], first_stage[c][:, :] if early else stage[:, 0:size], w_hi[:, cols].bitcast(F32),
                                  ALU.subtract).then_inc(w_lo_done, 1)

            split_x(0, 0, 0, 0)
            for c in range(SCAN_CHUNKS):
                split_weight_lo(c)

            def x2_transposed(t, par_x, s):
                wait(dve, x_lo_done, t + 1)
                dve.tensor_tensor(xin[par_x][:, :, s, :], ps_t[:, 0:KC * B].rearrange("p (k b) -> p k b", k=KC),
                                  xin[par_x][:, :, s, :], ALU.add).then_inc(x2T_done, 1)

            def unit_prod(g, u):
                n = U * g + u
                wait(dve, act1_done, n + 1)
                wait(dve, l1a_ready, 2 * n + 2)
                dve.tensor_tensor(act_1, act_1, ps_l1[1][:, :], ALU.mult).then_inc(prod1_done, 1)

            def add_part(g):
                wait(dve, ld_part, 16 * (g + 1))
                wait(dve, l2a_ready, U * g + U)
                for j in range(2):
                    two = part[:, j * N:(j + 1) * N]
                    last = dve.scalar_tensor_tensor(two, ps_l2[j][:, :], 1.0 / 8, two, ALU.mult, ALU.add)
                last.then_inc(part_done, 1)

            def over_experts(ap):
                return ap.to_broadcast([B, S, E_RT])

            class Chain:
                n = 0

            def link(g, ins):
                Chain.n += 1
                ins.then_inc(router_step, 1)
                wait(dve, router_step, ROUTER_STEPS * g + Chain.n)

            def best_two(g):
                Chain.n = 0
                wait(dve, sig_done, g + 1)
                link(g, dve.tensor_tensor(score[:, :, :], s_r[:, :, :], over_experts(r_bias[:, :].unsqueeze(1)), ALU.add))
                dve.sem_inc(router_go, 1)
                for s in range(S):
                    Chain.n += 1
                    dve.max(best[:, s, :], score[:, s, :]).then_inc(router_step, 1)
                wait(dve, router_step, ROUTER_STEPS * g + Chain.n)
                dve.sem_inc(router_go, 1)
                for s in range(S):
                    Chain.n += 1
                    dve.max_index(best_i[:, s, :], best[:, s, :], score[:, s, :]).then_inc(router_step, 1)

            def make_masks(g):
                wait(dve, router_step, ROUTER_STEPS * g + Chain.n)
                link(g, dve.tensor_copy(expert[:, :, :], best_i[:, :, 0:K2]))
                for k in range(K2):
                    Chain.n += 1
                    dve.tensor_tensor(mask[k][:, :, :], over_experts(iota8[:, :].unsqueeze(1)),
                                      over_experts(expert[:, :, k:k + 1]), ALU.is_equal).then_inc(router_step, 1)
                Chain.n += 1
                dve.tensor_copy(seen[:, 0, :], seen[:, S, :]).then_inc(router_step, 1)
                wait(dve, router_step, ROUTER_STEPS * g + Chain.n)
                link(g, dve.tensor_tensor(both[:, :, :], mask[0][:, :, :], mask[1][:, :, :], ALU.add))
                for s in range(S - 1):
                    link(g, dve.tensor_tensor(seen[:, s + 1, :], seen[:, s, :], both[:, s, :], ALU.add))
                dve.tensor_tensor(seen[:, S, :], seen[:, S - 1, :], both[:, S - 1, :], ALU.add).then_inc(masks_done, 1)

            def read_places(g):
                wait(dve, pos_ready, g + 1)
                dve.tensor_copy(pos[:, :, :], ps_t[:, POS].rearrange("b (s e) -> b s e", s=S)).then_inc(pos_done, 1)

            def group_rows(ap, g):
                return ap[:, g * S:(g + 1) * S, :] if is_static(g) else ap[:, bass.ds(g * S, S), :]

            def rows(g, par):
                wait(dve, pos_done, g + 1)
                for k in range(K2):
                    Chain.n += 1
                    dve.tensor_tensor(tmp[k][:, :, :], mask[k][:, :, :], pos[:, :, :], ALU.mult).then_inc(router_step, 1)
                wait(dve, router_step, ROUTER_STEPS * g + Chain.n)
                for k in range(K2):
                    Chain.n += 1
                    dve.tensor_reduce(place[:, :, k], tmp[k][:, :, :], AX.X, ALU.add).then_inc(router_step, 1)
                wait(dve, router_step, ROUTER_STEPS * g + Chain.n)
                dve.scalar_tensor_tensor(idx_x[par][:, :, :], expert[:, :, :], float(REGION), place[:, :, :], ALU.mult, ALU.add)\
                    .then_inc(idx_done, 1)
                dve.tensor_copy(group_rows(place_all, g), place[:, :, :]).then_inc(idx_done, 1)
                dve.tensor_copy(group_rows(expert_all, g), expert[:, :, :]).then_inc(idx_done, 1)

            def picks(g):
                for k in range(K2):
                    Chain.n += 1
                    dve.tensor_tensor(tmp[k][:, :, :], mask[k][:, :, :], s_r[:, :, :], ALU.mult).then_inc(router_step, 1)
                wait(dve, router_step, ROUTER_STEPS * g + Chain.n)
                for k in range(K2):
                    Chain.n += 1
                    dve.tensor_reduce(picked[:, :, k], tmp[k][:, :, :], AX.X, ALU.add).then_inc(router_step, 1)
                wait(dve, router_step, ROUTER_STEPS * g + Chain.n)
                link(g, dve.tensor_tensor(denom[:, :], picked[:, :, 0], picked[:, :, 1], ALU.add))

            def gates(g):
                Chain.n += 3
                dve.tensor_scalar(valid[:, :], denom[:, :], DENOM_MIN, None, ALU.is_gt).then_inc(router_step, 1)
                dve.tensor_scalar(evenly[:, :], denom[:, :], DENOM_MIN, 0.125, ALU.is_le, ALU.mult).then_inc(router_step, 1)
                dve.tensor_scalar(recip[:, :], denom[:, :], DENOM_MIN, None, ALU.add).then_inc(router_step, 1)
                wait(dve, router_step, ROUTER_STEPS * g + Chain.n)
                link(g, dve.reciprocal(denom[:, :], recip[:, :]))
                link(g, dve.scalar_tensor_tensor(recip[:, :], denom[:, :], 0.25, valid[:, :], ALU.mult, ALU.mult))
                link(g, dve.tensor_tensor(picked[:, :, :], picked[:, :, :], recip[:, :].unsqueeze(2).to_broadcast([B, S, K2]), ALU.mult))
                link(g, dve.tensor_tensor(group_rows(gate_all, g), picked[:, :, :], evenly[:, :].unsqueeze(2).to_broadcast([B, S, K2]), ALU.add))

            def read_logits(g):
                wait(dve, zr_ready, S * g + S)
                dve.tensor_tensor(z_r[:, :, :], ps_t[:, ZR].rearrange("p (s e) -> p s e", s=S),
                                  over_experts(z_cond[:, :].unsqueeze(1)), ALU.add).then_inc(zr_done, 1)

            def scan_body(g, half, par):
                started = not (is_static(g) and g == 0)
                for s in range(S):
                    t = S * g + s
                    if started or s > 0:
                        x2_transposed(t - 1, par if s > 0 else 1 - par, (s - 1) % S)
                    if s < S - 1:
                        split_x(t + 1, half, par, s + 1)
                    elif not (is_static(g) and g == G - 1):
                        split_x(t + 1, half + par, 1 - par, 0)
                    wait(dve, tanh_done, t + 1)
                    wait(dve, hw_ready, t + 1)
                    dve.scalar_tensor_tensor(mem[:, :], tanh_g[:, 0:C], 1.0, ps_w[:, HW], ALU.add, ALU.mult).then_inc(v_done, 1)
                    wait(dve, v_done, t + 1)
                    dve.scalar_tensor_tensor(mem[:, :], mem[:, :], 0.5, ps_w[:, XW], ALU.mult, ALU.add).then_inc(mem_done, 1)
                    dve.scalar_tensor_tensor(keep[:, :], tanh_g[:, C:2 * C], 1.0, h[:, :], ALU.add, ALU.mult).then_inc(keep_done, 1)
                    dve.tensor_scalar(renew[:, :], tanh_g[:, C:2 * C], -0.5, 0.5, ALU.mult, ALU.add).then_inc(renew_done, 1)
                    if s == 0 and started:
                        read_logits(g - 1)
                    if s == 3 and started:
                        wait(dve, zr_ready, t)
                        read_places(g - 1)
                    wait(dve, cand_done, t + 1)
                    wait(dve, renew_done, 2 * t + 1)
                    dve.tensor_tensor(renew[:, :], renew[:, :], cand[:, :], ALU.mult).then_inc(renew_done, 1)
                    wait(dve, renew_done, 2 * t + 2)
                    wait(dve, x2_row_done, t)
                    dve.scalar_tensor_tensor(h[:, :], keep[:, :], 0.5, renew[:, :], ALU.mult, ALU.add).then_inc(h_done, 1)
                    if s == 0 and started:
                        split_weight_lo(g + EARLY_CHUNKS - 1)
                    if not started and s < SH_CHUNKS:
                        split_weight_lo(SCAN_CHUNKS + s)
                    if s == 1 and not (is_static(g) and g < 2):
                        add_part(g - 2)
                    if s == 1 and started:
                        best_two(g - 1)
                    if s == 2 and started:
                        make_masks(g - 1)
                        picks(g - 1)
                    if s == 3 and started:
                        rows(g - 1, 1 - par)
                        gates(g - 1)
                    wait(dve, hT_ready, t + 1)
                    dve.tensor_copy(hT_hi, ps_t[:, 0:KC * B]).then_inc(hT_hi_done, 1)
                    wait(dve, hT_hi_done, t + 2)
                    dve.tensor_tensor(hT_lo, ps_t[:, 0:KC * B], hT_hi.bitcast(F32), ALU.subtract).then_inc(hT_lo_done, 1)
                    if started:
                        unit_prod(g - 1, s)

            groups(dve, scan_body)
            x2_transposed(T - 1, 1, S - 1)
            read_logits(G - 1)
            best_two(G - 1)
            make_masks(G - 1)
            read_places(G - 1)
            dve.wait_ge(x2_row_done, T)
            rows(G - 1, 1)
            add_part(G - 2)
            picks(G - 1)
            gates(G - 1)
            assert Chain.n == ROUTER_STEPS, Chain.n

            step = [0]

            def then(ins):
                step[0] += 1
                ins.then_inc(table_step, 1)
                dve.wait_ge(table_step, step[0])

            dve.wait_ge(count_ready, 1)
            then(dve.tensor_copy(count[:, :], ps_c[:, 0:E_RT]))
            dve.wait_ge(tile_i_done, 1)
            dve.tensor_tensor(pad_at[:, :], count[0:1, :], region_of[0:1, :], ALU.add).then_inc(pad_done, 1)
            then(dve.tensor_scalar(count_i[:, :], count[:, :], float(TILE - 1), None, ALU.add))
            then(dve.tensor_scalar(count_i[:, :], count_i[:, :], TILE.bit_length() - 1, None, ALU.arith_shift_right))
            then(dve.tensor_copy(tiles_of[:, :], count_i[:, :]))
            then(dve.tensor_copy(tiles_to[:, 0:1], tiles_of[:, 0:1]))
            for e in range(1, E_RT):
                then(dve.tensor_tensor(tiles_to[:, e:e + 1], tiles_to[:, e - 1:e], tiles_of[:, e:e + 1], ALU.add))
            then(dve.tensor_tensor(y_base[:, :], tiles_to[:, :], tiles_of[:, :], ALU.subtract))
            then(dve.tensor_scalar(y_base[:, :], y_base[:, :], float(TILE), None, ALU.mult))
            then(dve.tensor_scalar(skip_rows[:, :], tiles_of[:, :], -float(TILE), float(REGION), ALU.mult, ALU.add))
            then(dve.tensor_copy(tile_f, tile_i))
            then(dve.tensor_scalar(acc_r, tile_f, float(TILE), None, ALU.mult))
            then(dve.tensor_scalar(acc_e, tile_f, 0.0, None, ALU.mult))
            for e in range(E_RT):
                then(dve.tensor_scalar(past, tile_f, tiles_to[0:1, e:e + 1], None, ALU.is_ge))
                then(dve.tensor_tensor(acc_e, acc_e, past, ALU.add))
                then(dve.scalar_tensor_tensor(acc_r, past, skip_rows[0:1, e:e + 1], acc_r, ALU.mult, ALU.add))
            then(dve.tensor_copy(tile_x, acc_r))
            then(dve.tensor_scalar(acc_e, acc_e, float(E_RT - 1), float(CHUNK), ALU.min, ALU.mult))
            dve.tensor_scalar(tile_w, acc_e, float(RT_BASE), None, ALU.add).then_inc(table_done, 1)

            for u in range(U):
                unit_prod(G - 1, u)
            add_part(G - 1)

            def rows_lo(i, q):
                wait(dve, xt_hi_done, i + 1)
                wait(dve, hid_ready, i - 1)
                dve.tensor_tensor(xt_lo[q % 2], ps_xt[q % 2][:, :], xt_hi[q % 2].bitcast(F32), ALU.subtract).then_inc(xt_lo_done, 1)

            def hidden_split(i, q):
                wait(dve, ht_ready, i + 1)
                wait(dve, y_ready, i - 1)
                dve.tensor_copy(hid_hi[q % 2], ps_ht[q % 2][:, :]).then_inc(ht_hi_done, 1)
                wait(dve, ht_hi_done, i + 1)
                dve.tensor_tensor(hid_lo[q % 2], ps_ht[q % 2][:, :], hid_hi[q % 2].bitcast(F32), ALU.subtract).then_inc(ht_lo_done, 1)

            def slot(i, jj, q):
                if not is_static(i) or i < TILES:
                    rows_lo(i, q)
                if not is_static(i) or 2 <= i:
                    hidden_split(i - 2, (q - 2) % 4)

            for i in range(4):
                slot(i, 0, i)

            n = 1
            dve.tensor_copy(y_at, place_all[:, :, :]).then_inc(y_idx_step, 1)
            for e in range(E_RT):
                dve.wait_ge(y_idx_step, n)
                dve.tensor_scalar(y_off, expert_all[:, :, :], float(e), y_base[:, e:e + 1], ALU.is_equal, ALU.mult)\
                    .then_inc(y_idx_step, 1)
                dve.wait_ge(y_idx_step, n + 1)
                dve.tensor_tensor(y_at, y_at, y_off, ALU.add).then_inc(y_idx_step, 1)
                n += 2
            dve.wait_ge(y_idx_step, n)
            dve.tensor_copy(idx_y, y_at).then_inc(y_idx_done, 1)

            with dve.Fori(1, TILES // 4) as jj:
                for q in range(4):
                    slot(4 * jj + q, jj, q)
            for i in range(TILES, TILES + 2):
                slot(i, 0, i % 4)

            def x2_lo_of(g, par):
                wait(dve, x2_hi_done, g + 1)
                dve.tensor_tensor(x2_lo[par], x2_in[:, :], x2_hi[par].bitcast(F32), ALU.subtract).then_inc(x2_lo_done, 1)

            x2_lo_of(0, 0)

            OUT_STEPS = 2 + S * K2

            def output_shared(g, half, par):
                wait(dve, l2_ready, U * g + U)
                wait(dve, ld_res[par], 16 * (half + 1))
                wait(dve, out_step, OUT_STEPS * g)
                gates = gate_all[:, g * S:(g + 1) * S, :] if is_static(g) else gate_all[:, bass.ds(g * S, S), :]
                dve.tensor_copy(gate_cur, gates).then_inc(gate_cur_done, 1)
                for j in range(2):
                    two = res[par][:, 2 * j:2 * j + 2, :].rearrange("b s c -> b (s c)")
                    dve.scalar_tensor_tensor(two, ps_o[par][j][:, :], 1.0 / 8, two, ALU.mult, ALU.add).then_inc(out_step, 1)

            def output_routed(g, half, par, k):
                if k == 0:
                    wait(dve, gate_cur_done, g + 1)
                    wait(dve, gathered[par], 16 * S * K2 * (half + 1))
                wait(dve, out_step, OUT_STEPS * g + 2 + S * k)
                for s in range(S):
                    dve.scalar_tensor_tensor(res[par][:, s, :], got[par][k][:, s, :], gate_cur[:, s, k:k + 1],
                                             res[par][:, s, :], ALU.mult, ALU.add).then_inc(out_step, 1)
                if k == K2 - 1:
                    wait(dve, out_step, OUT_STEPS * (g + 1))
                    dve.sem_inc(out_done, 1)

            def shared_body(g, half, par):
                for u in range(U):
                    n = U * g + u
                    wait(dve, act_done, n + 1)
                    wait(dve, l1_ready, 2 * n + 2)
                    dve.tensor_tensor(act_out[u % 2], act_out[u % 2], ring[2 * (u % 2) + 1][:, :], ALU.mult).then_inc(prod_done, 1)
                    wait(dve, hi_done, n + 1)
                    dve.tensor_tensor(prod_lo[u % 2], act_out[u % 2], prod_hi[u % 2].bitcast(F32), ALU.subtract).then_inc(lo_done, 1)
                    if u == 2 and not (is_static(g) and g == G - 1):
                        x2_lo_of(g + 1, 1 - par)
                    if not (is_static(g) and g == 0):
                        before_it = (g - 1, half - (1 - par), 1 - par)
                        if u == 1:
                            output_shared(*before_it)
                        if u == 2:
                            output_routed(*before_it, 0)
                        if u == 3:
                            output_routed(*before_it, 1)

            groups(dve, shared_body)
            output_shared(G - 1, G // 2 - 1, 1)
            output_routed(G - 1, G // 2 - 1, 1, 0)
            output_routed(G - 1, G // 2 - 1, 1, 1)

        @block.gpsimd
        def _(pool):
            pool.memset(zeros[:, :], 0.0).then_inc(zeros_done, 1)
            pool.memset(ident[:, :], 0.0).then_inc(pool_step, 1)
            pool.memset(row0[:, :], 0.0).then_inc(pool_step, 1)
            pool.memset(ones[:, :], 1.0).then_inc(pool_step, 1)
            pool.iota(iota_i[:, :], pattern=[[1, E_RT]], base=0, channel_multiplier=0).then_inc(pool_step, 1)
            pool.wait_ge(pool_step, 4)
            pool.tensor_copy(iota8[:, :], iota_i[:, :]).then_inc(pool_step, 1)
            pool.tensor_scalar(region_of[:, :], iota_i[:, :], float(REGION), None, ALU.mult).then_inc(pool_step, 1)
            pool.wait_ge(pool_step, 6)
            pool.affine_select(out=ident[:, :], in_=ident[:, :], compare_op=ALU.not_equal, fill=1.0, base=0,
                               pattern=[[-1, P]], channel_multiplier=1).then_inc(const_done, 1)
            pool.affine_select(out=row0[:, :], in_=row0[:, :], compare_op=ALU.not_equal, fill=1.0, base=0,
                               pattern=[[0, 1]], channel_multiplier=1).then_inc(const_done, 1)
            pool.affine_select(out=before[:, :], in_=ones[:, :], compare_op=ALU.is_gt, fill=0.0, base=0,
                               pattern=[[1, P]], channel_multiplier=-1).then_inc(const_done, 1)

            def add_row(g, half, par, s):
                t = S * g + s
                wait(pool, h_done, t + 1)
                if s % 2 == 0:
                    wait(pool, ld_row[s // 2], 16 * (g + 1))
                if s == 0:
                    wait(pool, st_x2[par], 16 * half)
                wait(pool, scattered[par * S + s], 16 * K2 * half)
                pool.tensor_tensor(x2_row[par][:, s, :], x_row[s // 2][:, s % 2, :], h[:, :], ALU.add).then_inc(x2_row_done, 1)

            def group_lo(g, par):
                wait(pool, grp_hi_done, 2 * g + 2)
                pool.tensor_tensor(grp_lo, buf[par][:, :], grp_hi.bitcast(F32), ALU.subtract).then_inc(grp_lo_done, 1)

            def unit_lo(g, u):
                wait(pool, hi1_done, U * g + u + 1)
                pool.tensor_tensor(prod1_lo, act_1, prod1_hi.bitcast(F32), ALU.subtract).then_inc(lo1_done, 1)

            def scatter(par, s):
                for k in range(K2):
                    pool.indirect_dma_start(out=rows_x, out_offset=bass.IndirectOffsetOnAxis(ap=idx_x[par][:, s, k:k + 1], axis=0),
                                            in_=x2_row[par][:, s, :], in_offset=None).then_inc(scattered[par * S + s], 16)

            def scan_body(g, half, par):
                for s in range(S):
                    if s == 0 and not (is_static(g) and g == 0):
                        group_lo(g - 1, 1 - par)
                    add_row(g, half, par, s)
                    if s < 2 and not (is_static(g) and g < 2):
                        scatter(par, 2 + s)
                    if s == 3 and not (is_static(g) and g < 1):
                        wait(pool, idx_done, 3 * g)
                        pool.sem_inc(pool_go, 1)
                        scatter(1 - par, 0)
                        scatter(1 - par, 1)
                    if not (is_static(g) and g == 0):
                        unit_lo(g - 1, s)

            groups(pool, scan_body)
            group_lo(G - 1, 1)
            scatter(0, 2)
            scatter(0, 3)
            pool.wait_ge(x2_row_done, T)
            pool.iota(tile_i, pattern=[[1, TILES]], base=0, channel_multiplier=0).then_inc(tile_i_done, 1)
            pool.wait_ge(idx_done, 3 * G)
            for s in range(S):
                scatter(1, s)
            for u in range(U):
                unit_lo(G - 1, u)

            for q in range(4):
                pool.wait_ge(st_t[q], 16 * TILES // 4)
            pool.wait_ge(y_idx_done, 1)

            def shared_body(g, half, par):
                wait(pool, gathered[par], 16 * S * K2 * half)
                cur = idx_y[:, g * S:(g + 1) * S, :] if is_static(g) else idx_y[:, bass.ds(g * S, S), :]
                pool.tensor_copy(idx_y_cur[par], cur).then_inc(idx_cur_done, 1)
                wait(pool, idx_cur_done, g + 1)
                wait(pool, out_done, g - 1)
                pool.sem_inc(pool_go, 1)
                for k, s in ((k, s) for k in range(K2) for s in range(S)):
                    pool.indirect_dma_start(out=got[par][k][:, s, :], out_offset=None, in_=rows_y,
                                            in_offset=bass.IndirectOffsetOnAxis(ap=idx_y_cur[par][:, s, k:k + 1], axis=0))\
                        .then_inc(gathered[par], 16)

            groups(pool, shared_body)


_INS = ["x", "xT", "condT", "cond", "wall", "biases", "wrT", "rbias"]


def _layout(i):
    import numpy as np
    a = {k: np.asarray(v) for k, v in i.items()}

    def tiles(w):
        return w.reshape(-1, P, w.shape[1]).transpose(1, 0, 2).reshape(P, -1)

    def shared(e):
        for f in range(F_SH // P):
            rows = slice(f * P, (f + 1) * P)
            yield from (tiles(a["L1_cond_s_w1"][e, rows].T), tiles(a["L1_cond_s_w3"][e, rows].T), a["L1_cond_s_w2"][e][:, rows].T)

    parts = [tiles(a["L0_cond_w_W"]), tiles(a["L0_cond_wx_W"]), tiles(a["L0_cond_wh_W"]), *shared(0)]
    for e in range(E_RT):
        parts += [tiles(a["L1_cond_r_w1"][e].T), tiles(a["L1_cond_r_w2"][e].T)]
    parts += shared(1)
    wall = np.concatenate(parts, axis=1)
    return {
        "x": a["x"].reshape(B, T * C),
        "xT": a["x"].reshape(B, G, S, KC, P).transpose(1, 4, 3, 2, 0).reshape(G, P, KC * S * B),
        "condT": a["cond_1024"].reshape(B, KC, P).transpose(2, 1, 0).reshape(P, KC * B),
        "cond": a["cond_1024"],
        "wall": wall,
        "biases": np.concatenate([a["L0_cond_w_b"], a["L0_cond_wx_b"], a["L0_cond_wh_b"]])[None],
        "wrT": a["L1_cond_W_router"].reshape(E_RT, 2 * KC, P).transpose(2, 1, 0),
        "rbias": a["L1_cond_router_bias"],
    }


def kernel(**inputs):
    import numpy as _np
    import concourse.bacc as _bacc
    from concourse import mybir as _mybir
    from concourse.bass_utils import run_bass_kernel_spmd as _run

    nc = _bacc.Bacc("TRN2", target_bir_lowering=False, num_devices=1)
    laid = _layout(inputs)
    arrays, args = {}, []
    for name in _INS:
        a = _np.ascontiguousarray(laid[name])
        arrays[f"in_{name}"] = a
        args.append(nc.dram_tensor(f"in_{name}", a.shape, _mybir.dt.from_np(a.dtype), kind="ExternalInput").ap())
    args.append(nc.dram_tensor("out", (B, T * C), _mybir.dt.float32, kind="ExternalOutput").ap())
    build(nc, *args)
    r = _run(nc, [arrays], core_ids=[0])
    return r.results[0]["out"].reshape(B, T, C)
```

```python
import concourse.bass as bass
from concourse import mybir
from contextlib import ExitStack

F32 = mybir.dt.float32
F32R = mybir.dt.float32r
U32 = mybir.dt.uint32
I32 = mybir.dt.int32
ACT = mybir.ActivationFunctionType
ALU = mybir.AluOpType
AX = mybir.AxisListType

P = 128
B, T, C = 128, 64, 256
KC = C // P
S = 4
N = S * B
G = T // S
TOKENS = B * T
K2 = 2
F_SH = 512
E_RT, F_RT = 8, 256
KF = F_RT // P
U = F_SH // P
LAG = 2
UNIT_COLS = 3 * KC * P
RW = C + E_RT
W_GATES = 0
W_X = W_GATES + 2 * KC * 2 * C
W_H = W_X + KC * RW
CHUNK = KC * F_RT + KF * C
RT_BASE = W_H + KC * RW + U * UNIT_COLS
SH_BASE = (W_H + KC * RW, RT_BASE + E_RT * CHUNK)
COLS = SH_BASE[1] + U * UNIT_COLS
SCAN_PIECES = 4
EARLY = ((0, 1024), (1024, 1024), (W_X, KC * RW), (W_H, KC * RW),
         *((SH_BASE[0] + i * 1024, 1024) for i in range(3)))
EARLY_PIECES = len(EARLY)
PIECE = 768
PIECES = EARLY_PIECES + G - 1


def piece(c):
    if isinstance(c, int) and c < EARLY_PIECES:
        return EARLY[c]
    first = RT_BASE + (c - EARLY_PIECES) * PIECE
    return first, COLS - first if isinstance(c, int) and c == PIECES - 1 else PIECE


DENOM_MIN = 1e-9

R = 2
TILE = R * P
TILES = K2 * TOKENS // TILE + E_RT
REGION = TOKENS + TILE
EMPTY = E_RT
ROWS_X = E_RT * REGION + E_RT * TILE


def build(nc, x, xT, condT, cond, wall, biases, wrT, rbias, out):
    rows_x = nc.dram_tensor("rows_x", [ROWS_X, C], F32, kind="Internal").ap()
    rows_y = nc.dram_tensor("rows_y", [TILES * TILE, C], F32, kind="Internal").ap()
    x2_d = nc.dram_tensor("x2_d", [G, B, S * C], F32, kind="Internal").ap()
    x2T_d = nc.dram_tensor("x2T_d", [G, P, KC * N], F32, kind="Internal").ap()
    part_d = nc.dram_tensor("part_d", [G, B, S * C], F32, kind="Internal").ap()
    ctx = ExitStack()
    with ctx:
        def sb(name, shape, dt=F32):
            return ctx.enter_context(nc.sbuf_tensor(name, shape, dt))

        def sem(name):
            return ctx.enter_context(nc.semaphore(name))

        w_hi = sb("w_hi", [P, COLS], F32R)
        w_lo = sb("w_lo", [P, COLS], F32R)
        ident = sb("ident", [P, P])
        before = sb("before", [P, P])
        ones = sb("ones", [P, P])

        buf = [sb(f"buf{i}", [P, S * C]) for i in range(8)]
        rbuf = [sb(f"rbuf{i}", [P, S * C], F32R) for i in range(4)]
        rhalf = [sb(f"rhalf{i}", [P, N], F32R) for i in range(4)]

        xin = [buf[i][:, :].rearrange("p (k s b) -> p k s b", k=KC, s=S) for i in range(2)]
        x_row = [buf[2][:, i * 2 * C:(i + 1) * 2 * C].rearrange("b (s c) -> b s c", s=2) for i in range(2)]
        part, last_part = buf[3], buf[2]
        x2_row = [buf[4 + i][:, :].rearrange("b (s c) -> b s c", s=S) for i in range(2)]
        stage = buf[6][:, :]
        first_stage = (buf[6], buf[3], buf[7], buf[5], buf[6], buf[3], buf[5])
        act_1 = buf[7][:, 0:N]
        grp_hi, grp_lo = rbuf[0][:, :], rbuf[1][:, :]
        x_hi = rbuf[2][:, 0:C].rearrange("p (k b) -> p k b", k=KC)
        x_lo = rbuf[2][:, C:2 * C].rearrange("p (k b) -> p k b", k=KC)
        hT_hi = rbuf[2][:, 2 * C:3 * C]
        hT_lo = rbuf[2][:, 3 * C:4 * C]
        bias_z = buf[7][:, 2 * C:4 * C]
        bias_w = sb("bias_w", [P, 2, RW])
        prod1_hi, prod1_lo = (rhalf[0], rhalf[2]), (rhalf[1], rhalf[3])
        condT_sb = buf[4][:, 0:C]
        h = sb("h", [B, C])
        tanh_g = sb("tanh_g", [B, 2 * C])
        wb = sb("wb", [B, 2, RW])
        mem = wb[:, 1, 0:C]
        cand = sb("cand", [B, C])
        keep = sb("keep", [B, C])
        renew = tanh_g[:, C:2 * C]
        wr_sb = sb("wr_sb", [P, 2 * KC, E_RT])
        r_bias = sb("r_bias", [B, E_RT])
        iota_i = sb("iota_i", [B, E_RT], I32)
        iota8 = sb("iota8", [B, E_RT])
        z_r = [sb(f"z_r{i}", [B, S, E_RT]) for i in range(2)]
        s_r = sb("s_r", [B, S, E_RT])
        score = sb("score", [B, S, E_RT])
        best = sb("best", [B, S, 8])
        best_i = sb("best_i", [B, S, 8], U32)
        expert = sb("expert", [B, S, K2])
        mask = [sb(f"mask{k}", [B, S, E_RT]) for k in range(K2)]
        both = sb("both", [B, S, E_RT])
        seen = sb("seen", [B, S + 1, E_RT])
        pos = sb("pos", [B, S, E_RT])
        tmp = [sb(f"tmp{k}", [B, S, E_RT]) for k in range(K2)]
        place = sb("place", [B, S, K2])
        picked = sb("picked", [B, S, K2])
        denom = sb("denom", [B, S])
        valid = sb("valid", [B, S])
        recip = sb("recip", [B, S])
        evenly = sb("evenly", [B, S])
        idx_x = [sb(f"idx_x{i}", [B, S, K2], U32) for i in range(2)]
        expert_all = sb("expert_all", [B, T, K2])
        place_all = sb("place_all", [B, T, K2])
        gate_all = sb("gate_all", [B, T, K2])
        zeros = sb("zeros", [P, C])
        count = sb("count", [P, E_RT])
        count_i = sb("count_i", [P, E_RT], I32)
        pad_at = sb("pad_at", [1, E_RT], I32)
        region_of = sb("region_of", [P, E_RT])
        tiles_of = sb("tiles_of", [P, E_RT])
        tiles_to = sb("tiles_to", [P, E_RT])
        y_base = sb("y_base", [P, E_RT])
        skip_rows = sb("skip_rows", [P, E_RT])
        tile_x = cand[:, :].bitcast(I32)[0:1, 0:TILES]
        tile_w = keep[:, :].bitcast(I32)[0:1, 0:TILES]
        tile_i = wb[:, 0, :].bitcast(I32)[0:1, 0:TILES]
        xt = [buf[i // 2][:, i % 2 * R * C:(i % 2 + 1) * R * C] for i in range(4)]
        yt = [buf[2 + i // 2][:, i % 2 * R * C:(i % 2 + 1) * R * C] for i in range(4)]
        hid = [buf[4][:, i * R * F_RT:(i + 1) * R * F_RT] for i in range(2)]
        xt_hi = [rbuf[0][:, i * R * C:(i + 1) * R * C] for i in range(2)]
        xt_lo = [rbuf[1][:, i * R * C:(i + 1) * R * C] for i in range(2)]
        w1_hi, w1_lo = (rhalf[0], rhalf[2]), (rhalf[1], rhalf[3])
        hid_hi = [rbuf[2][:, i * R * F_RT:(i + 1) * R * F_RT] for i in range(2)]
        hid_lo = [rbuf[3][:, i * R * F_RT:(i + 1) * R * F_RT] for i in range(2)]
        y_at = buf[7][:, 2 * C:2 * C + T * K2].rearrange("b (t k) -> b t k", k=K2)
        y_off = buf[7][:, 3 * C:3 * C + T * K2].rearrange("b (t k) -> b t k", k=K2)
        tile_f = buf[6][0:1, 0:TILES]
        acc_e = buf[6][0:1, TILES:2 * TILES]
        acc_r = buf[6][0:1, 2 * TILES:3 * TILES]
        past = buf[6][0:1, 3 * TILES:(3 + E_RT) * TILES].rearrange("p (t e) -> p t e", e=E_RT)
        res = [buf[i][:, :].rearrange("b (s c) -> b s c", s=S) for i in range(2)]
        got = [[buf[2 + 2 * i + k][:, :].rearrange("b (s c) -> b s c", s=S) for k in range(K2)] for i in range(2)]
        act_out = [buf[6][:, i * N:(i + 1) * N] for i in range(2)]
        x2_in = buf[7]
        x2_hi = [rbuf[0][:, :], rbuf[2][:, :]]
        x2_lo = [rbuf[1][:, :], rbuf[3][:, :]]
        prod_hi = [rhalf[i][:, :] for i in range(2)]
        prod_lo = [rhalf[2 + i][:, :] for i in range(2)]
        old = tanh_g[:, :].bitcast(U32)
        idx_y = old[:, 0:T * K2].rearrange("b (t k) -> b t k", k=K2)
        idx_y_cur = [old[:, (T + i * S) * K2:(T + i * S + S) * K2].rearrange("b (t k) -> b t k", k=K2) for i in range(2)]
        gate_cur = tanh_g[:, C:C + S * K2].rearrange("b (t k) -> b t k", k=K2)

        pair = ctx.enter_context(nc.psum_tensor("pair", [P, 2 * N], F32))
        bank = [ctx.enter_context(nc.psum_tensor(f"bank{i}", [P, N], F32)) for i in (0, 2, 4, 5, 6, 7)]
        bank = [bank[0], pair[:, 0:N], bank[1], pair[:, N:2 * N], *bank[2:]]
        ps_z, ps_t = bank[0], bank[2]
        ps_x, ps_s = bank[1][:, 0:RW], bank[3][:, 0:RW]
        ps_w = pair[:, :].rearrange("p (a n) -> p a n", a=2)[:, :, 0:RW]
        POS = slice(KC * B, KC * B + S * E_RT)
        ps_l1, ps_l2 = bank[4:6], bank[6:8]
        ps_c = ps_t[:, POS.stop:POS.stop + E_RT]
        ps_xt, ps_h, ps_y = bank[0:2], bank[2:4], bank[6:8]
        ring, ps_o = (bank[0], bank[1], bank[2], bank[5]), (bank[3:5], bank[6:8])

        ld_const = sem("ld_const")
        ld_condT = sem("ld_condT")
        ld_early = [sem(f"ld_early{i}") for i in range(EARLY_PIECES)]
        ld_w = sem("ld_w")
        st_x2T = sem("st_x2T")
        ld_part = sem("ld_part")
        ld_last_part = sem("ld_last_part")
        sp_go = sem("sp_go")
        st_part = sem("st_part")
        ld_x = [sem(f"ld_x{i}") for i in range(2)]
        ld_row = [sem(f"ld_row{i}") for i in range(2)]
        st_x2 = [sem(f"st_x2{i}") for i in range(2)]
        scattered = [sem(f"scattered{i}") for i in range(2 * S)]
        pads = sem("pads")
        st_empty = sem("st_empty")
        ld_t = [sem(f"ld_t{i}") for i in range(4)]
        st_t = [sem(f"st_t{i}") for i in range(4)]
        ld_res = [sem(f"ld_res{i}") for i in range(2)]
        gathered = [sem(f"gathered{i}") for i in range(2)]
        st_out = [sem(f"st_out{i}") for i in range(2)]
        pool_step = sem("pool_step")
        const_done = sem("const_done")
        bias_done = sem("bias_done")
        w_hi_done = sem("w_hi_done")
        w_lo_done = sem("w_lo_done")
        zc_ready = sem("zc_ready")
        zc_done = sem("zc_done")
        x_hi_done = sem("x_hi_done")
        x_lo_done = sem("x_lo_done")
        xpart_ready = sem("xpart_ready")
        z_ready = sem("z_ready")
        hw_ready = sem("hw_ready")
        zb_done = sem("zb_done")
        wb_done = sem("wb_done")
        tanh_done = sem("tanh_done")
        v_done = sem("v_done")
        mem_done = sem("mem_done")
        cand_done = sem("cand_done")
        keep_done = sem("keep_done")
        renew_done = sem("renew_done")
        h_done = sem("h_done")
        hT_ready = sem("hT_ready")
        hT_hi_done = sem("hT_hi_done")
        hT_lo_done = sem("hT_lo_done")
        x2T_done = sem("x2T_done")
        x2_row_done = sem("x2_row_done")
        zr_ready = sem("zr_ready")
        zx_done = sem("zx_done")
        zh_done = sem("zh_done")
        sig_done = sem("sig_done")
        router_go = sem("router_go")
        pool_go = sem("pool_go")
        router_step = sem("router_step")
        masks_done = sem("masks_done")
        pos_ready = sem("pos_ready")
        pos_done = sem("pos_done")
        idx_done = sem("idx_done")
        grp_hi_done = sem("grp_hi_done")
        grp_lo_done = sem("grp_lo_done")
        part_done = sem("part_done")
        l1a_ready = sem("l1a_ready")
        act1_done = sem("act1_done")
        prod1_done = sem("prod1_done")
        hi1_done = sem("hi1_done")
        lo1_done = sem("lo1_done")
        l2a_ready = sem("l2a_ready")
        count_ready = sem("count_ready")
        table_step = sem("table_step")
        pad_done = sem("pad_done")
        zeros_done = sem("zeros_done")
        tile_i_done = sem("tile_i_done")
        table_done = sem("table_done")
        xt_ready = sem("xt_ready")
        xt_hi_done = sem("xt_hi_done")
        xt_lo_done = sem("xt_lo_done")
        hid_ready = sem("hid_ready")
        hid_done = sem("hid_done")
        w1_done = sem("w1_done")
        hid_hi_done = sem("hid_hi_done")
        hid_lo_done = sem("hid_lo_done")
        y_ready = sem("y_ready")
        y_done = sem("y_done")
        l1_ready = sem("l1_ready")
        act_done = sem("act_done")
        prod_done = sem("prod_done")
        hi_done = sem("hi_done")
        lo_done = sem("lo_done")
        l2_ready = sem("l2_ready")
        ld_x2T = sem("ld_x2T")
        x2_hi_done = sem("x2_hi_done")
        x2_lo_done = sem("x2_lo_done")
        y_idx_step = sem("y_idx_step")
        y_idx_done = sem("y_idx_done")
        idx_cur_done = sem("idx_cur_done")
        gate_cur_done = sem("gate_cur_done")
        out_step = sem("out_step")
        out_done = sem("out_done")

        def wait(eng, s, value):
            if not (isinstance(value, int) and value <= 0):
                eng.wait_ge(s, value)

        def is_static(g):
            return isinstance(g, int)

        ROUTER_STEPS = 1 + S + S + 1 + K2 + 1 + 1 + (S - 1) + 4 * K2 + 1 + 3 + 4

        block = ctx.enter_context(nc.Block())

        def groups(eng, body):
            body(0, 0, 0)
            body(1, 0, 1)
            with eng.Fori(1, G // 2 - 1) as j:
                body(2 * j, j, 0)
                body(2 * j + 1, j, 1)
            body(G - 2, G // 2 - 1, 0)
            body(G - 1, G // 2 - 1, 1)

        @block.sync
        def _(sp):
            def load_early(c):
                first, size = piece(c)
                sp.dma_start(first_stage[c][:, 0:size], wall[:, first:first + size]).then_inc(ld_early[c], 16)

            load_early(0)
            sp.dma_start(buf[0][:, :], xT[0]).then_inc(ld_x[0], 16)
            sp.dma_start(condT_sb, condT).then_inc(ld_condT, 16)
            load_early(1)
            load_early(2)
            load_early(3)
            sp.dma_start(buf[1][:, :], biases.partition_broadcast(P)).then_inc(ld_const, 16)
            sp.dma_start(wr_sb[:, :, :], wrT).then_inc(ld_const, 16)
            sp.dma_start(h[:, :], cond).then_inc(ld_const, 16)
            sp.dma_start(r_bias[:, :], rbias.partition_broadcast(B)).then_inc(ld_const, 16)
            for i in range(2):
                sp.dma_start(x_row[i].rearrange("b s c -> b (s c)"), x[:, i * 2 * C:(i + 1) * 2 * C]).then_inc(ld_row[i], 16)
            sp.wait_ge(bias_done, 2)
            sp.dma_start(buf[1][:, :], xT[1]).then_inc(ld_x[1], 16)
            for c, before_it in ((4, 0), (5, 1), (6, 3)):
                sp.wait_ge(w_lo_done, before_it + 1)
                load_early(c)
            sp.wait_ge(zeros_done, 1)
            sp.dma_start(rows_x[EMPTY * REGION:ROWS_X, :].rearrange("(p j) c -> p j c", p=P),
                         zeros[:, :].unsqueeze(1).to_broadcast([P, R * E_RT, C])).then_inc(st_empty, 16)

            def pick(ap, g):
                return ap[g] if is_static(g) else ap[bass.ds(g, 1)].rearrange("a p n -> (a p) n")

            def load_rows(g, i):
                at = (g * S + 2 * i) * C
                sp.dma_start(x_row[i].rearrange("b s c -> b (s c)"),
                             x[:, at:at + 2 * C] if is_static(g) else x[:, bass.ds(at, 2 * C)]).then_inc(ld_row[i], 16)

            def store_part(g):
                wait(sp, part_done, g + 1)
                src = last_part if is_static(g) and g == G - 1 else part
                sp.dma_start(pick(part_d, g), src[:, :]).then_inc(st_part, 16)

            def load_part(g, stored):
                wait(sp, st_part, 16 * g)
                sp.sem_inc(sp_go, 1)
                if is_static(g) and g == 0:
                    sp.wait_ge(w_lo_done, EARLY_PIECES)
                wait(sp, *stored)
                sp.dma_start(part[:, :], pick(x2_d, g)).then_inc(ld_part, 16)

            def scan_body(g, half, par):
                started = not (is_static(g) and g == 0)
                more = not (is_static(g) and g == G - 1)
                if started:
                    wait(sp, x2T_done, S * g)
                    sp.dma_start(pick(x2T_d, g - 1), buf[1 - par][:, :]).then_inc(st_x2T, 16)
                if more:
                    wait(sp, x2_row_done, S * g + 2)
                    load_rows(g + 1, 0)
                if started and more:
                    wait(sp, st_x2T, 16 * g)
                    wait(sp, grp_lo_done, g)
                    sp.dma_start(buf[1 - par][:, :], pick(xT, g + 1)).then_inc(ld_x[1 - par], 16)
                if not (is_static(g) and g < 2):
                    store_part(g - 2)
                if started:
                    load_part(g - 1, (st_x2[1 - par], 16 * (half + par)))
                if more:
                    wait(sp, w_lo_done, g + EARLY_PIECES if started else 5)
                    first, size = piece(g + EARLY_PIECES)
                    sp.dma_start(stage[:, 0:size], wall[:, first:first + size] if is_static(g) else wall[:, bass.ds(first, size)])                      .then_inc(ld_w, 16)
                wait(sp, x2_row_done, S * g + S)
                if more:
                    load_rows(g + 1, 1)
                sp.dma_start(pick(x2_d, g), buf[4 + par][:, :]).then_inc(st_x2[par], 16)

            groups(sp, scan_body)
            sp.wait_ge(x2T_done, T)
            sp.dma_start(x2T_d[G - 1], buf[1][:, :]).then_inc(st_x2T, 16)
            sp.wait_ge(st_x2[1], 16 * G // 2)
            sp.dma_start(last_part[:, :], x2_d[G - 1]).then_inc(ld_last_part, 16)

            sp.wait_ge(pad_done, 1)
            for e in range(E_RT):
                row = sp.value_load(pad_at[0:1, e:e + 1], min_val=e * REGION, max_val=e * REGION + TOKENS)
                sp.dma_start(rows_x[bass.ds(row, TILE), :].rearrange("(p r) c -> p r c", r=R),
                             zeros[:, :].unsqueeze(1).to_broadcast([P, R, C])).then_inc(pads, 16)
            store_part(G - 2)
            sp.wait_ge(st_empty, 16)
            sp.wait_ge(st_x2T, 16 * G)
            sp.wait_ge(grp_lo_done, G)
            sp.wait_ge(zr_ready, 1)
            sp.wait_ge(table_done, 1)
            for i in range(2 * S):
                sp.wait_ge(scattered[i], 16 * K2 * G // 2)
            sp.wait_ge(pads, 16 * E_RT)

            def load_tile(i, jj, q):
                wait(sp, xt_ready, i - 3)
                row = sp.value_load(tile_x[0:1, bass.ds(i, 1)], min_val=0, max_val=ROWS_X - TILE)
                sp.dma_start(xt[q], rows_x[bass.ds(row, TILE), :].rearrange("(p r) c -> p (r c)", r=R)).then_inc(ld_t[q], 16)

            def store_tile(i, q):
                wait(sp, y_done, i + 1)
                dst = rows_y[i * TILE:(i + 1) * TILE, :] if is_static(i) else rows_y[bass.ds(i * TILE, TILE), :]
                sp.dma_start(dst.rearrange("(p r) c -> p (r c)", r=R), yt[q]).then_inc(st_t[q], 16)

            BEHIND = 6
            for i in range(8):
                load_tile(i, i // 4, i % 4)
                if i == 3:
                    store_part(G - 1)
                if i >= BEHIND:
                    store_tile(i - BEHIND, (i - BEHIND) % 4)
            with sp.Fori(2, TILES // 4) as jj:
                for q in range(4):
                    load_tile(4 * jj + q, jj, q)
                    store_tile(4 * jj + (q - BEHIND), (q - BEHIND) % 4)
            sp.wait_ge(y_idx_done, 1)
            sp.dma_start(x2_in[:, :], x2T_d[0]).then_inc(ld_x2T, 16)
            for i in range(TILES, TILES + BEHIND):
                store_tile(i - BEHIND, (i - BEHIND) % 4)

            sp.wait_ge(st_part, 16 * G)
            sp.wait_ge(xt_ready, TILES)

            def store_out(g, par):
                wait(sp, out_done, g + 1)
                dst = out[:, g * S * C:(g + 1) * S * C] if is_static(g) else out[:, bass.ds(g * (S * C), S * C)]
                sp.dma_start(dst, buf[par][:, :]).then_inc(st_out[par], 16)

            def shared_body(g, half, par):
                if not (is_static(g) and g == G - 1):
                    wait(sp, x2_lo_done, g + 1)
                    sp.dma_start(x2_in[:, :], pick(x2T_d, g + 1)).then_inc(ld_x2T, 16)
                if not (is_static(g) and g < 2):
                    store_out(g - 2, par)
                    wait(sp, st_out[par], 16 * half)
                sp.dma_start(buf[par][:, :], pick(part_d, g)).then_inc(ld_res[par], 16)

            groups(sp, shared_body)
            store_out(G - 2, 0)
            store_out(G - 1, 1)
            for par in range(2):
                sp.wait_ge(st_out[par], 16 * G // 2)

        @block.tensor
        def _(pe):
            def three_state(out, hi, lo, w_col, n, start, stop):
                last = None
                for i, (a, w) in enumerate(((hi, w_hi), (hi, w_lo), (lo, w_hi))):
                    cols = slice(w_col, w_col + n) if is_static(w_col) else bass.ds(w_col, n)
                    last = pe.matmul(out, a, w[:, cols], start=start and i == 0, stop=stop and i == 2)
                return last

            def x_part(t):
                wait(pe, x_lo_done, t + 1)
                wait(pe, zb_done, t)
                for k in range(KC):
                    three_state(ps_z[:, :], x_hi[:, k, :], x_lo[:, k, :], W_GATES + k * 2 * C, 2 * C, k == 0, False)
                wait(pe, wb_done, t)
                if is_static(t) and t == 0:
                    pe.wait_ge(w_lo_done, 3)
                for k in range(KC):
                    last = three_state(ps_x, x_hi[:, k, :], x_lo[:, k, :], W_X + k * RW, RW, k == 0, k == KC - 1)
                last.then_inc(xpart_ready, 1)

            def h_part(t):
                wait(pe, hT_hi_done, t + 1)
                for k in range(KC):
                    hs = slice(k * B, (k + 1) * B)
                    w = slice(W_GATES + (KC + k) * 2 * C, W_GATES + (KC + k + 1) * 2 * C)
                    pe.matmul(ps_z[:, :], hT_hi[:, hs], w_hi[:, w], start=False, stop=False)
                    pe.matmul(ps_z[:, :], hT_hi[:, hs], w_lo[:, w], start=False, stop=False)
                wait(pe, hT_lo_done, t + 1)
                for k in range(KC):
                    hs = slice(k * B, (k + 1) * B)
                    w = slice(W_GATES + (KC + k) * 2 * C, W_GATES + (KC + k + 1) * 2 * C)
                    last = pe.matmul(ps_z[:, :], hT_lo[:, hs], w_hi[:, w], start=False, stop=k == KC - 1)
                last.then_inc(z_ready, 1)
                wait(pe, wb_done, t)
                if is_static(t) and t == 0:
                    pe.wait_ge(w_lo_done, SCAN_PIECES)
                for k in range(KC):
                    hs = slice(k * B, (k + 1) * B)
                    last = three_state(ps_s, hT_hi[:, hs], hT_lo[:, hs], W_H + k * RW, RW, k == 0, k == KC - 1)
                last.then_inc(hw_ready, 1)

            def last_router():
                wait(pe, x2T_done, T)
                for k in range(KC):
                    last = pe.matmul(ps_c, xin[1][:, k, S - 1, :], wr_sb[:, k, :], start=k == 0, stop=k == KC - 1)
                last.then_inc(zr_ready, 1)

            def layer1(dst, base, hi, lo):
                for k in range(KC):
                    for i, (w, xx) in enumerate(((w_hi, hi), (w_lo, hi), (w_hi, lo))):
                        last = pe.matmul(dst[:, :], w[:, base + k * P:base + (k + 1) * P], xx[:, k * N:(k + 1) * N],
                                         start=k == 0 and i == 0, stop=k == KC - 1 and i == 2)
                return last

            def layer2(dst, expert, u, hi, lo, steps=range(S)):
                col = SH_BASE[expert] + u * UNIT_COLS + 2 * KC * P
                for s in steps:
                    hs = slice(s * B, (s + 1) * B)
                    half_bank = slice(s % 2 * C, (s % 2 + 1) * C)
                    for i, (a, w) in enumerate(((hi, w_hi), (hi, w_lo), (lo, w_hi))):
                        last = pe.matmul(dst[s // 2][:, half_bank], a[:, hs], w[:, col:col + C],
                                         start=u == 0 and s % 2 == 0 and i == 0, stop=u == U - 1 and i == 2,
                                         skip_group_check=True)
                return last

            def unit_layer1(g, u):
                n = U * g + u
                wait(pe, grp_lo_done, g + 1)
                for which, used in enumerate((act1_done, prod1_done)):
                    wait(pe, used, n)
                    layer1(ps_l1[which], SH_BASE[0] + u * UNIT_COLS + which * KC * P, grp_hi, grp_lo).then_inc(l1a_ready, 1)

            def unit_layer2(g, u, bank_of):
                if bank_of == 0:
                    wait(pe, lo1_done, U * g + u + 1)
                    if u == 0:
                        wait(pe, part_done, g)
                last = layer2(ps_l2, 0, u, prod1_hi[u % 2], prod1_lo[u % 2], (2 * bank_of, 2 * bank_of + 1))
                if bank_of == 1:
                    last.then_inc(l2a_ready, 1)

            def unit_before(g, s, bank_of):
                if s > 0 and not (is_static(g) and g == 0):
                    unit_layer2(g - 1, s - 1, bank_of)
                if s == 0 and not (is_static(g) and g < 2):
                    unit_layer2(g - 2, U - 1, bank_of)

            def places(g):
                wait(pe, masks_done, g + 1)
                pe.matmul(ps_t[:, POS], before[:, :], both[:, :, :].rearrange("b s e -> b (s e)"), start=True, stop=False)
                pe.matmul(ps_t[:, POS], ones[:, :], seen[:, 0:S, :].rearrange("b s e -> b (s e)"), start=False, stop=True)\
                  .then_inc(pos_ready, 1)

            def transpose_state(t):
                wait(pe, h_done, t + 1)
                wait(pe, x2T_done, t)
                for k in range(KC):
                    last = pe.transpose(ps_t[:, k * B:(k + 1) * B], h[:, k * P:(k + 1) * P], ident[:, :])
                last.then_inc(hT_ready, 1)

            pe.wait_ge(const_done, 3)
            pe.wait_ge(w_lo_done, 1)
            x_part(0)
            pe.wait_ge(ld_const, 4 * 16)
            for k in range(KC):
                last = pe.matmul(ps_c, condT_sb[:, k * B:(k + 1) * B], wr_sb[:, KC + k, :], start=k == 0, stop=k == KC - 1)
            last.then_inc(zc_ready, 1)

            def scan_body(g, half, par):
                for s in range(S):
                    t = S * g + s
                    h_part(t)
                    if s > 0:
                        unit_before(g, s - 1, 1)
                    elif not (is_static(g) and g == 0):
                        unit_before(g - 1, S - 1, 1)
                    if not (is_static(g) and t == T - 1):
                        x_part(t + 1)
                    if not (is_static(g) and g == 0):
                        if s == 0 and is_static(g) and g == 1:
                            pe.wait_ge(w_lo_done, EARLY_PIECES)
                        unit_layer1(g - 1, s)
                        if s == 2:
                            places(g - 1)
                    if s == 3:
                        wait(pe, pos_done, g)
                    transpose_state(t)
                    unit_before(g, s, 0)

            groups(pe, scan_body)
            last_router()
            unit_layer1(G - 1, 0)
            unit_before(G - 1, S - 1, 1)
            for i in range(2):
                unit_layer2(G - 2, U - 1, i)
            places(G - 1)
            pe.wait_ge(zh_done, T)
            pe.matmul(ps_c, ones[:, :], seen[:, S, :], start=True, stop=True).then_inc(count_ready, 1)
            for u in range(1, U):
                unit_layer1(G - 1, u)
                for i in range(2):
                    unit_layer2(G - 1, u - 1, i)
            for i in range(2):
                unit_layer2(G - 1, U - 1, i)

            pe.wait_ge(w_lo_done, PIECES)
            pe.wait_ge(table_done, 1)

            def weights_of(i):
                return pe.snap(pe.value_load(tile_w[0:1, bass.ds(i, 1)], min_val=RT_BASE, max_val=RT_BASE + (E_RT - 1) * CHUNK))

            def turn(out, rows):
                for k in range(KC):
                    for r in range(R):
                        last = pe.transpose(out[:, k * TILE + r * P:k * TILE + (r + 1) * P],
                                            rows[:, r * C + k * P:r * C + (k + 1) * P], ident[:, :])
                return last

            def product(out, hi, lo, col):
                for r in range(R):
                    for k in range(KC):
                        ks = slice(k * TILE + r * P, k * TILE + (r + 1) * P)
                        last = three_state(out[:, r * C:(r + 1) * C], hi[:, ks], lo[:, ks], col + k * C, C, k == 0, k == KC - 1)
                return last

            def turn_rows(i, q):
                wait(pe, xt_lo_done, i - 1)
                turn(ps_xt[q % 2], xt[q]).then_inc(xt_ready, 1)

            def first_layer(i, q):
                wait(pe, w1_done, i + 1)
                wait(pe, xt_lo_done, i + 1)
                wait(pe, hid_done, i - 1)
                whi, wlo = w1_hi[q % 2], w1_lo[q % 2]
                for f in range(KF):
                    for k in range(KC):
                        ws = slice(k * F_RT + f * P, k * F_RT + (f + 1) * P)
                        ks = slice(k * TILE, (k + 1) * TILE)
                        for n, (w, xx) in enumerate(((whi, xt_hi), (wlo, xt_hi), (whi, xt_lo))):
                            last = pe.matmul(ps_h[q % 2][:, f * TILE:(f + 1) * TILE], w[:, ws], xx[q % 2][:, ks],
                                             start=k == 0 and n == 0, stop=k == KC - 1 and n == 2)
                last.then_inc(hid_ready, 1)

            def second_layer(i, q, col):
                wait(pe, hid_lo_done, i + 1)
                wait(pe, y_done, i - 1)
                product(ps_y[q % 2], hid_hi[q % 2], hid_lo[q % 2], col + KC * F_RT).then_inc(y_ready, 1)

            def slot(i, jj, q):
                if not is_static(i) or 2 <= i:
                    col = weights_of(i - 2)
                if not is_static(i) or i < TILES:
                    wait(pe, ld_t[q], 16 * (jj + 1))
                    turn_rows(i, q)
                if not is_static(i) or 1 <= i <= TILES:
                    first_layer(i - 1, (q - 1) % 4)
                if not is_static(i) or 2 <= i:
                    second_layer(i - 2, (q - 2) % 4, col)

            for i in range(4):
                slot(i, 0, i)
            with pe.Fori(1, TILES // 4) as jj:
                for q in range(4):
                    slot(4 * jj + q, jj, q)
            for i in range(TILES, TILES + 2):
                slot(i, 0, i % 4)

            def shared_body(g, half, par):
                wait(pe, x2_lo_done, g + 1)
                if is_static(g) and g == 1:
                    pe.wait_ge(y_done, TILES)
                for u in range(U):
                    n = U * g + u
                    for which, used in enumerate((act_done, prod_done)):
                        wait(pe, used, n - 1)
                        layer1(ring[2 * (u % 2) + which], SH_BASE[1] + u * UNIT_COLS + which * KC * P,
                               x2_hi[par], x2_lo[par]).then_inc(l1_ready, 1)
                    if not (is_static(g) and g == 0 and u < LAG):
                        wait(pe, lo_done, n - LAG + 1)
                        if u == LAG:
                            wait(pe, out_done, g - 1)
                        layer2(ps_o[par if u >= LAG else 1 - par], 1, (u - LAG) % U, prod_hi[u % 2], prod_lo[u % 2]).then_inc(l2_ready, 1)

            groups(pe, shared_body)
            for u in range(U - LAG, U):
                wait(pe, lo_done, U * (G - 1) + u + 1)
                layer2(ps_o[1], 1, u, prod_hi[u % 2], prod_lo[u % 2]).then_inc(l2_ready, 1)

        @block.scalar
        def _(act):
            def weight_hi(c):
                early = is_static(c) and c < EARLY_PIECES
                if early:
                    act.wait_ge(ld_early[c], 16)
                else:
                    wait(act, ld_w, 16 * (c - EARLY_PIECES + 1))
                first, size = piece(c)
                dst = w_hi[:, first:first + size] if is_static(c) else w_hi[:, bass.ds(first, size)]
                act.activation(dst, first_stage[c][:, 0:size] if early else stage[:, 0:size], ACT.Copy).then_inc(w_hi_done, 1)

            def state_hi(t, src):
                act.activation(hT_hi, src, ACT.Copy).then_inc(hT_hi_done, 1)

            def x_hi_of(t, half, par_x, s):
                if s == 0:
                    wait(act, ld_x[par_x], 16 * (half + 1))
                wait(act, xpart_ready, t)
                act.activation(x_hi, xin[par_x][:, :, s, :], ACT.Copy).then_inc(x_hi_done, 1)

            weight_hi(0)
            x_hi_of(0, 0, 0, 0)
            act.wait_ge(ld_condT, 16)
            state_hi(-1, condT_sb)
            weight_hi(1)
            weight_hi(2)
            weight_hi(3)
            x_hi_of(1, 0, 0, 1)

            def scores(g, par):
                wait(act, zh_done, S * g + S)
                act.activation(s_r[:, :, :], z_r[par][:, :, :], ACT.Sigmoid).then_inc(sig_done, 1)

            def group_hi(g, par, last):
                wait(act, x2T_done, S * g + (S if last else S - 1))
                if not last:
                    wait(act, l1a_ready, 2 * U * g)
                steps = slice(S - 1, S) if last else slice(0, S - 1)
                act.activation(grp_hi.rearrange("p (k s b) -> p k s b", k=KC, s=S)[:, :, steps, :],
                               xin[par][:, :, steps, :], ACT.Copy).then_inc(grp_hi_done, 1)

            def unit_silu(g, u):
                n = U * g + u
                wait(act, l1a_ready, 2 * n + 1)
                wait(act, lo1_done, n)
                act.activation(act_1, ps_l1[0][:, :], ACT.Silu).then_inc(act1_done, 1)

            def unit_hi(g, u):
                n = U * g + u
                wait(act, prod1_done, n + 1)
                wait(act, l2a_ready, n - 1)
                act.activation(prod1_hi[u % 2][:, :], act_1, ACT.Copy).then_inc(hi1_done, 1)

            def scan_body(g, half, par):
                started = not (is_static(g) and g == 0)
                for s in range(S):
                    t = S * g + s
                    if s == 0 and started:
                        group_hi(g - 1, 1 - par, True)
                    wait(act, zb_done, t + 1)
                    act.activation(tanh_g[:, :], tanh_g[:, :], ACT.Tanh, scale=0.5).then_inc(tanh_done, 1)
                    wait(act, mem_done, t + 1)
                    act.activation(cand[:, :], mem, ACT.Tanh).then_inc(cand_done, 1)
                    if s == 0 and started:
                        scores(g - 1, 1 - par)
                    if not started and s < EARLY_PIECES - SCAN_PIECES:
                        weight_hi(SCAN_PIECES + s)
                    if s < S - 2:
                        x_hi_of(t + 2, half, par, s + 2)
                    elif not (is_static(g) and g == G - 1):
                        x_hi_of(t + 2, half + par, 1 - par, s + 2 - S)
                    if started:
                        unit_silu(g - 1, s)
                    wait(act, hT_ready, t + 1)
                    wait(act, z_ready, t + 1)
                    if not (is_static(t) and t == T - 1):
                        state_hi(t, ps_t[:, 0:KC * B])
                    if s == 0 and started:
                        weight_hi(g + EARLY_PIECES - 1)
                    if s == S - 1:
                        group_hi(g, par, False)
                    if started:
                        unit_hi(g - 1, s)

            groups(act, scan_body)
            group_hi(G - 1, 1, True)
            scores(G - 1, 1)
            for u in range(U):
                unit_silu(G - 1, u)
                unit_hi(G - 1, u)

            def rows_hi(i, q):
                wait(act, xt_ready, i + 1)
                wait(act, hid_ready, i - 1)
                act.activation(xt_hi[q % 2], ps_xt[q % 2][:, :], ACT.Copy).then_inc(xt_hi_done, 1)

            def gelu(i, q):
                wait(act, hid_ready, i + 1)
                wait(act, hid_lo_done, i - 1)
                act.activation(hid[q % 2], ps_h[q % 2][:, :], ACT.Gelu).then_inc(hid_done, 1)

            def y_out(i, jj, q):
                wait(act, y_ready, i + 1)
                wait(act, st_t[q], 16 * jj)
                act.activation(yt[q], ps_y[q % 2][:, :], ACT.Copy).then_inc(y_done, 1)

            def slot(i, jj, q):
                if not is_static(i) or i < TILES:
                    rows_hi(i, q)
                if not is_static(i) or 1 <= i <= TILES:
                    gelu(i - 1, (q - 1) % 4)
                if not is_static(i) or 2 <= i:
                    y_out(i - 2, jj - (1 if q < 2 else 0), (q - 2) % 4)

            def x2_hi_of(g, par):
                wait(act, ld_x2T, 16 * (g + 1))
                wait(act, l1_ready, 2 * U * (g - 1))
                act.activation(x2_hi[par], x2_in[:, :], ACT.Copy).then_inc(x2_hi_done, 1)

            for i in range(8):
                if i == 2:
                    act.wait_ge(st_part, 16 * G)
                slot(i, i // 4, i % 4)
            with act.Fori(2, TILES // 4) as jj:
                for q in range(4):
                    slot(4 * jj + q, jj, q)
            slot(TILES, TILES // 4, 0)
            act.wait_ge(hid_ready, TILES)
            x2_hi_of(0, 0)
            slot(TILES + 1, TILES // 4, 1)

            def shared_body(g, half, par):
                for u in range(U):
                    n = U * g + u
                    wait(act, l1_ready, 2 * n + 1)
                    wait(act, lo_done, n - 1)
                    act.activation(act_out[u % 2], ring[2 * (u % 2)][:, :], ACT.Silu).then_inc(act_done, 1)
                    if u == 2 and not (is_static(g) and g == G - 1):
                        x2_hi_of(g + 1, 1 - par)
                    wait(act, prod_done, n + 1)
                    wait(act, l2_ready, n - 1)
                    act.activation(prod_hi[u % 2], act_out[u % 2], ACT.Copy).then_inc(hi_done, 1)

            groups(act, shared_body)

        @block.vector
        def _(dve):
            dve.memset(seen[:, :, :], 0.0).then_inc(const_done, 1)

            def split_weight_lo(c):
                wait(dve, w_hi_done, c + 1)
                early = is_static(c) and c < EARLY_PIECES
                first, size = piece(c)
                cols = slice(first, first + size) if is_static(c) else bass.ds(first, size)
                dve.tensor_tensor(w_lo[:, cols], first_stage[c][:, 0:size] if early else stage[:, 0:size], w_hi[:, cols].bitcast(F32),
                                  ALU.subtract).then_inc(w_lo_done, 1)

            split_weight_lo(0)
            split_weight_lo(1)
            dve.wait_ge(hT_hi_done, 1)
            dve.tensor_tensor(hT_lo, condT_sb, hT_hi.bitcast(F32), ALU.subtract).then_inc(hT_lo_done, 1)
            split_weight_lo(2)
            split_weight_lo(3)
            dve.wait_ge(w_lo_done, 3)
            dve.wait_ge(ld_const, 4 * 16)
            dve.tensor_copy(bias_z, buf[1][:, 0:2 * C]).then_inc(bias_done, 1)
            dve.tensor_copy(bias_w[:, :, 0:C], buf[1][:, 2 * C:4 * C].rearrange("p (a c) -> p a c", a=2)).then_inc(bias_done, 1)
            dve.memset(bias_w[:, 1, C:RW], 0.0).then_inc(bias_done, 1)
            dve.wait_ge(zc_ready, 1)
            dve.tensor_copy(bias_w[:, 0, C:RW], ps_c).then_inc(zc_done, 1)
            dve.wait_ge(bias_done, 3)
            dve.wait_ge(zc_done, 1)

            def x2_transposed(t, par_x, s):
                wait(dve, x_lo_done, t + 1)
                dve.tensor_tensor(xin[par_x][:, :, s, :], ps_t[:, 0:KC * B].rearrange("p (k b) -> p k b", k=KC),
                                  xin[par_x][:, :, s, :], ALU.add).then_inc(x2T_done, 1)

            def unit_prod(g, u):
                n = U * g + u
                wait(dve, act1_done, n + 1)
                wait(dve, l1a_ready, 2 * n + 2)
                dve.tensor_tensor(act_1, act_1, ps_l1[1][:, :], ALU.mult).then_inc(prod1_done, 1)

            def add_part(g):
                last_group = is_static(g) and g == G - 1
                wait(dve, *((ld_last_part, 16) if last_group else (ld_part, 16 * (g + 1))))
                wait(dve, l2a_ready, U * g + U)
                for j in range(2):
                    two = (last_part if last_group else part)[:, j * N:(j + 1) * N]
                    last = dve.scalar_tensor_tensor(two, ps_l2[j][:, :], 1.0 / 8, two, ALU.mult, ALU.add)
                last.then_inc(part_done, 1)

            def split_lo(done, hi_done, value, lo, src, hi):
                wait(dve, hi_done, value)
                dve.tensor_tensor(lo, src, hi.bitcast(F32), ALU.subtract).then_inc(done, 1)

            def split_unit(u):
                split_lo(lo1_done, hi1_done, U * (G - 1) + u + 1, prod1_lo[u % 2][:, :], act_1, prod1_hi[u % 2][:, :])

            def over_experts(ap):
                return ap.to_broadcast([B, S, E_RT])

            class Chain:
                n = 0

            def link(g, ins):
                Chain.n += 1
                ins.then_inc(router_step, 1)
                wait(dve, router_step, ROUTER_STEPS * g + Chain.n)

            def best_two(g):
                Chain.n = 0
                wait(dve, sig_done, g + 1)
                link(g, dve.tensor_tensor(score[:, :, :], s_r[:, :, :], over_experts(r_bias[:, :].unsqueeze(1)), ALU.add))
                dve.sem_inc(router_go, 1)
                for s in range(S):
                    Chain.n += 1
                    dve.max(best[:, s, :], score[:, s, :]).then_inc(router_step, 1)
                wait(dve, router_step, ROUTER_STEPS * g + Chain.n)
                dve.sem_inc(router_go, 1)
                for s in range(S):
                    Chain.n += 1
                    dve.max_index(best_i[:, s, :], best[:, s, :], score[:, s, :]).then_inc(router_step, 1)

            def make_masks(g):
                wait(dve, router_step, ROUTER_STEPS * g + Chain.n)
                link(g, dve.tensor_copy(expert[:, :, :], best_i[:, :, 0:K2]))
                for k in range(K2):
                    Chain.n += 1
                    dve.tensor_tensor(mask[k][:, :, :], over_experts(iota8[:, :].unsqueeze(1)),
                                      over_experts(expert[:, :, k:k + 1]), ALU.is_equal).then_inc(router_step, 1)
                Chain.n += 1
                dve.tensor_copy(seen[:, 0, :], seen[:, S, :]).then_inc(router_step, 1)
                wait(dve, router_step, ROUTER_STEPS * g + Chain.n)
                link(g, dve.tensor_tensor(both[:, :, :], mask[0][:, :, :], mask[1][:, :, :], ALU.add))
                for s in range(S - 1):
                    link(g, dve.tensor_tensor(seen[:, s + 1, :], seen[:, s, :], both[:, s, :], ALU.add))
                dve.tensor_tensor(seen[:, S, :], seen[:, S - 1, :], both[:, S - 1, :], ALU.add).then_inc(masks_done, 1)

            def read_places(g):
                wait(dve, pos_ready, g + 1)
                dve.tensor_copy(pos[:, :, :], ps_t[:, POS].rearrange("b (s e) -> b s e", s=S)).then_inc(pos_done, 1)

            def group_rows(ap, g):
                return ap[:, g * S:(g + 1) * S, :] if is_static(g) else ap[:, bass.ds(g * S, S), :]

            def rows(g, par):
                wait(dve, pos_done, g + 1)
                for k in range(K2):
                    Chain.n += 1
                    dve.tensor_tensor(tmp[k][:, :, :], mask[k][:, :, :], pos[:, :, :], ALU.mult).then_inc(router_step, 1)
                wait(dve, router_step, ROUTER_STEPS * g + Chain.n)
                for k in range(K2):
                    Chain.n += 1
                    dve.tensor_reduce(place[:, :, k], tmp[k][:, :, :], AX.X, ALU.add).then_inc(router_step, 1)
                wait(dve, router_step, ROUTER_STEPS * g + Chain.n)
                dve.scalar_tensor_tensor(idx_x[par][:, :, :], expert[:, :, :], float(REGION), place[:, :, :], ALU.mult, ALU.add)\
                    .then_inc(idx_done, 1)
                dve.tensor_copy(group_rows(place_all, g), place[:, :, :]).then_inc(idx_done, 1)
                dve.tensor_copy(group_rows(expert_all, g), expert[:, :, :]).then_inc(idx_done, 1)

            def picks(g):
                for k in range(K2):
                    Chain.n += 1
                    dve.tensor_tensor(tmp[k][:, :, :], mask[k][:, :, :], s_r[:, :, :], ALU.mult).then_inc(router_step, 1)
                wait(dve, router_step, ROUTER_STEPS * g + Chain.n)
                for k in range(K2):
                    Chain.n += 1
                    dve.tensor_reduce(picked[:, :, k], tmp[k][:, :, :], AX.X, ALU.add).then_inc(router_step, 1)
                wait(dve, router_step, ROUTER_STEPS * g + Chain.n)
                link(g, dve.tensor_tensor(denom[:, :], picked[:, :, 0], picked[:, :, 1], ALU.add))

            def gates(g):
                Chain.n += 3
                dve.tensor_scalar(valid[:, :], denom[:, :], DENOM_MIN, None, ALU.is_gt).then_inc(router_step, 1)
                dve.tensor_scalar(evenly[:, :], denom[:, :], DENOM_MIN, 0.125, ALU.is_le, ALU.mult).then_inc(router_step, 1)
                dve.tensor_scalar(recip[:, :], denom[:, :], DENOM_MIN, None, ALU.add).then_inc(router_step, 1)
                wait(dve, router_step, ROUTER_STEPS * g + Chain.n)
                link(g, dve.reciprocal(denom[:, :], recip[:, :]))
                link(g, dve.scalar_tensor_tensor(recip[:, :], denom[:, :], 0.25, valid[:, :], ALU.mult, ALU.mult))
                link(g, dve.tensor_tensor(picked[:, :, :], picked[:, :, :], recip[:, :].unsqueeze(2).to_broadcast([B, S, K2]), ALU.mult))
                link(g, dve.tensor_tensor(group_rows(gate_all, g), picked[:, :, :], evenly[:, :].unsqueeze(2).to_broadcast([B, S, K2]), ALU.add))

            def logits(t, par, s):
                if not (is_static(t) and t == T - 1):
                    dve.tensor_copy(z_r[par][:, s, :], wb[:, 0, C:RW]).then_inc(zx_done, 1)
                if not (is_static(t) and t == 0):
                    wait(dve, zx_done, t)
                    row = z_r[par if s > 0 else 1 - par][:, (s - 1) % S, :]
                    dve.tensor_tensor(row, row, wb[:, 1, C:RW], ALU.add).then_inc(zh_done, 1)

            def scan_body(g, half, par):
                started = not (is_static(g) and g == 0)
                for s in range(S):
                    t = S * g + s
                    if started or s > 0:
                        x2_transposed(t - 1, par if s > 0 else 1 - par, (s - 1) % S)
                    wait(dve, z_ready, t + 1)
                    wait(dve, h_done, t)
                    dve.tensor_tensor(tanh_g[:, :], ps_z[:, :], bias_z, ALU.add).then_inc(zb_done, 1)
                    wait(dve, hw_ready, t + 1)
                    wait(dve, mem_done, t)
                    wait(dve, zh_done, t - 1)
                    dve.tensor_tensor(wb[:, :, :], ps_w, bias_w[:, :, :], ALU.add).then_inc(wb_done, 1)
                    wait(dve, tanh_done, t + 1)
                    wait(dve, wb_done, t + 1)
                    dve.scalar_tensor_tensor(mem, tanh_g[:, 0:C], 1.0, wb[:, 1, 0:C], ALU.add, ALU.mult).then_inc(v_done, 1)
                    wait(dve, v_done, t + 1)
                    dve.scalar_tensor_tensor(mem, mem, 0.5, wb[:, 0, 0:C], ALU.mult, ALU.add).then_inc(mem_done, 1)
                    dve.scalar_tensor_tensor(keep[:, :], tanh_g[:, C:2 * C], 1.0, h[:, :], ALU.add, ALU.mult).then_inc(keep_done, 1)
                    dve.tensor_scalar(renew, tanh_g[:, C:2 * C], -0.5, 0.5, ALU.mult, ALU.add).then_inc(renew_done, 1)
                    logits(t, par, s)
                    if s == 3 and started:
                        read_places(g - 1)
                    wait(dve, cand_done, t + 1)
                    wait(dve, renew_done, 2 * t + 1)
                    dve.tensor_tensor(renew, renew, cand[:, :], ALU.mult).then_inc(renew_done, 1)
                    wait(dve, renew_done, 2 * t + 2)
                    wait(dve, x2_row_done, t)
                    dve.scalar_tensor_tensor(h[:, :], keep[:, :], 0.5, renew, ALU.mult, ALU.add).then_inc(h_done, 1)
                    if not started and s < EARLY_PIECES - SCAN_PIECES:
                        split_weight_lo(SCAN_PIECES + s)
                    if s == 1 and not (is_static(g) and g < 2):
                        add_part(g - 2)
                    if s == 1 and started:
                        best_two(g - 1)
                    if s == 2 and started:
                        make_masks(g - 1)
                        picks(g - 1)
                    if s == 3 and started:
                        rows(g - 1, 1 - par)
                        if not (is_static(g) and g == G - 1):
                            gates(g - 1)
                    if not (is_static(t) and t == T - 1):
                        wait(dve, hT_hi_done, t + 2)
                        dve.tensor_tensor(hT_lo, ps_t[:, 0:KC * B], hT_hi.bitcast(F32), ALU.subtract).then_inc(hT_lo_done, 1)
                    if started:
                        unit_prod(g - 1, s)
                    if s == 0 and started:
                        split_weight_lo(g + EARLY_PIECES - 1)

            groups(dve, scan_body)
            dve.wait_ge(hT_ready, T)
            x2_transposed(T - 1, 1, S - 1)
            split_lo(grp_lo_done, grp_hi_done, 2 * G, grp_lo, buf[1][:, :], grp_hi)
            gates(G - 2)
            dve.wait_ge(zr_ready, 1)
            dve.tensor_tensor(z_r[1][:, S - 1, :], ps_c, bias_w[:, 0, C:RW], ALU.add).then_inc(zh_done, 1)
            best_two(G - 1)
            make_masks(G - 1)
            unit_prod(G - 1, 0)
            dve.wait_ge(count_ready, 1)
            read_places(G - 1)
            dve.wait_ge(x2_row_done, T)
            rows(G - 1, 1)

            split_unit(0)

            step = [0]

            def then(ins):
                step[0] += 1
                ins.then_inc(table_step, 1)
                dve.wait_ge(table_step, step[0])

            then(dve.tensor_copy(count[:, :], ps_c))
            dve.wait_ge(tile_i_done, 1)
            dve.tensor_tensor(pad_at[:, :], count[0:1, :], region_of[0:1, :], ALU.add).then_inc(pad_done, 1)
            add_part(G - 2)
            unit_prod(G - 1, 1)
            picks(G - 1)
            gates(G - 1)
            assert Chain.n == ROUTER_STEPS, Chain.n
            split_unit(1)
            then(dve.tensor_scalar(count_i[:, :], count[:, :], float(TILE - 1), None, ALU.add))
            then(dve.tensor_scalar(count_i[:, :], count_i[:, :], TILE.bit_length() - 1, None, ALU.arith_shift_right))
            then(dve.tensor_copy(tiles_of[:, :], count_i[:, :]))
            then(dve.tensor_copy(tiles_to[:, 0:1], tiles_of[:, 0:1]))
            for e in range(1, E_RT):
                then(dve.tensor_tensor(tiles_to[:, e:e + 1], tiles_to[:, e - 1:e], tiles_of[:, e:e + 1], ALU.add))
            then(dve.tensor_tensor(y_base[:, :], tiles_to[:, :], tiles_of[:, :], ALU.subtract))
            then(dve.tensor_scalar(y_base[:, :], y_base[:, :], float(TILE), None, ALU.mult))
            then(dve.tensor_scalar(skip_rows[:, :], tiles_of[:, :], -float(TILE), float(REGION), ALU.mult, ALU.add))
            unit_prod(G - 1, 2)
            then(dve.tensor_copy(tile_f, tile_i))
            then(dve.tensor_tensor(past, tile_f.unsqueeze(2).to_broadcast([1, TILES, E_RT]),
                                   tiles_to[0:1, :].unsqueeze(1).to_broadcast([1, TILES, E_RT]), ALU.is_ge))
            then(dve.tensor_reduce(acc_e, past, AX.X, ALU.add))
            then(dve.tensor_tensor(past, past, skip_rows[0:1, :].unsqueeze(1).to_broadcast([1, TILES, E_RT]), ALU.mult))
            split_unit(2)
            then(dve.tensor_reduce(acc_r, past, AX.X, ALU.add))
            then(dve.scalar_tensor_tensor(tile_x, tile_f, float(TILE), acc_r, ALU.mult, ALU.add))
            then(dve.tensor_scalar(acc_e, acc_e, float(E_RT - 1), float(CHUNK), ALU.min, ALU.mult))
            dve.tensor_scalar(tile_w, acc_e, float(RT_BASE), None, ALU.add).then_inc(table_done, 1)
            unit_prod(G - 1, U - 1)
            split_unit(U - 1)
            add_part(G - 1)

            dve.wait_ge(w_lo_done, PIECES)
            dve.wait_ge(table_done, 1)

            def rows_lo(i, q):
                wait(dve, xt_hi_done, i + 1)
                wait(dve, hid_ready, i - 1)
                dve.tensor_tensor(xt_lo[q % 2], ps_xt[q % 2][:, :], xt_hi[q % 2].bitcast(F32), ALU.subtract).then_inc(xt_lo_done, 1)

            def copy_w1(i, q):
                if is_static(i) and i < 2:
                    dve.wait_ge(l2a_ready, U * G - 1 + i)
                col = dve.snap(dve.value_load(tile_w[0:1, bass.ds(i, 1)], min_val=RT_BASE, max_val=RT_BASE + (E_RT - 1) * CHUNK))
                wait(dve, hid_ready, i - 1)
                for dst, w in ((w1_hi, w_hi), (w1_lo, w_lo)):
                    last = dve.tensor_copy(dst[q % 2][:, :], w[:, bass.ds(col, KC * F_RT)])
                last.then_inc(w1_done, 1)

            def hidden_split(i, q):
                wait(dve, hid_done, i + 1)
                wait(dve, y_ready, i - 1)
                dve.tensor_copy(hid_hi[q % 2], hid[q % 2]).then_inc(hid_hi_done, 1)
                wait(dve, hid_hi_done, i + 1)
                dve.tensor_tensor(hid_lo[q % 2], hid[q % 2], hid_hi[q % 2].bitcast(F32), ALU.subtract).then_inc(hid_lo_done, 1)

            def slot(i, jj, q):
                if not is_static(i) or i < TILES:
                    copy_w1(i, q)
                    rows_lo(i, q)
                if not is_static(i) or 1 <= i:
                    hidden_split(i - 1, (q - 1) % 4)

            for i in range(4):
                slot(i, 0, i)

            with dve.Fori(1, TILES // 4) as jj:
                for q in range(4):
                    slot(4 * jj + q, jj, q)
            slot(TILES, 0, 0)

            def x2_lo_of(g, par):
                wait(dve, x2_hi_done, g + 1)
                dve.tensor_tensor(x2_lo[par], x2_in[:, :], x2_hi[par].bitcast(F32), ALU.subtract).then_inc(x2_lo_done, 1)

            x2_lo_of(0, 0)

            OUT_STEPS = 2 + S * K2

            def take_gates(g, half, par):
                wait(dve, ld_res[par], 16 * (half + 1))
                wait(dve, out_step, OUT_STEPS * g)
                gates = gate_all[:, g * S:(g + 1) * S, :] if is_static(g) else gate_all[:, bass.ds(g * S, S), :]
                dve.tensor_copy(gate_cur, gates).then_inc(gate_cur_done, 1)

            def add_shared(g, par, n):
                wait(dve, l2_ready, U * g + U)
                if n > 0:
                    wait(dve, out_step, OUT_STEPS * g + n)
                for j in range(2):
                    two = res[par][:, 2 * j:2 * j + 2, :].rearrange("b s c -> b (s c)")
                    dve.scalar_tensor_tensor(two, ps_o[par][j][:, :], 1.0 / 8, two, ALU.mult, ALU.add).then_inc(out_step, 1)

            def add_routed(g, half, par, k, n):
                if k == 0:
                    wait(dve, gate_cur_done, g + 1)
                    wait(dve, gathered[par], 16 * S * K2 * (half + 1))
                if n > 0:
                    wait(dve, out_step, OUT_STEPS * g + n)
                for s in range(S):
                    dve.scalar_tensor_tensor(res[par][:, s, :], got[par][k][:, s, :], gate_cur[:, s, k:k + 1],
                                             res[par][:, s, :], ALU.mult, ALU.add).then_inc(out_step, 1)

            def finish(g):
                wait(dve, out_step, OUT_STEPS * (g + 1))
                dve.sem_inc(out_done, 1)

            def shared_body(g, half, par):
                for u in range(U):
                    n = U * g + u
                    wait(dve, act_done, n + 1)
                    wait(dve, l1_ready, 2 * n + 2)
                    dve.tensor_tensor(act_out[u % 2], act_out[u % 2], ring[2 * (u % 2) + 1][:, :], ALU.mult).then_inc(prod_done, 1)
                    wait(dve, hi_done, n + 1)
                    dve.tensor_tensor(prod_lo[u % 2], act_out[u % 2], prod_hi[u % 2].bitcast(F32), ALU.subtract).then_inc(lo_done, 1)
                    if u == 2 and not (is_static(g) and g == G - 1):
                        x2_lo_of(g + 1, 1 - par)
                    if not (is_static(g) and g == 0):
                        before_it = (g - 1, half - (1 - par), 1 - par)
                        if u == 1:
                            take_gates(*before_it)
                            add_shared(g - 1, 1 - par, 0)
                        if u >= 2:
                            add_routed(*before_it, u - 2, 2 + S * (u - 2))
                        if u == 3:
                            finish(g - 1)

            groups(dve, shared_body)
            last_one = (G - 1, G // 2 - 1, 1)
            take_gates(*last_one)
            for k in range(K2):
                add_routed(*last_one, k, S * k)
            add_shared(G - 1, 1, S * K2)
            finish(G - 1)

        @block.gpsimd
        def _(pool):
            pool.memset(zeros[:, :], 0.0).then_inc(zeros_done, 1)
            pool.memset(ident[:, :], 0.0).then_inc(pool_step, 1)
            pool.memset(ones[:, :], 1.0).then_inc(pool_step, 1)
            pool.iota(iota_i[:, :], pattern=[[1, E_RT]], base=0, channel_multiplier=0).then_inc(pool_step, 1)
            pool.wait_ge(pool_step, 3)
            pool.tensor_copy(iota8[:, :], iota_i[:, :]).then_inc(pool_step, 1)
            pool.tensor_scalar(region_of[:, :], iota_i[:, :], float(REGION), None, ALU.mult).then_inc(pool_step, 1)
            pool.wait_ge(pool_step, 5)
            pool.affine_select(out=ident[:, :], in_=ident[:, :], compare_op=ALU.not_equal, fill=1.0, base=0,
                               pattern=[[-1, P]], channel_multiplier=1).then_inc(const_done, 1)
            pool.affine_select(out=before[:, :], in_=ones[:, :], compare_op=ALU.is_gt, fill=0.0, base=0,
                               pattern=[[1, P]], channel_multiplier=-1).then_inc(const_done, 1)

            def x_lo_of(t, par_x, s):
                wait(pool, x_hi_done, t + 1)
                wait(pool, xpart_ready, t)
                pool.tensor_tensor(x_lo, xin[par_x][:, :, s, :], x_hi.bitcast(F32), ALU.subtract).then_inc(x_lo_done, 1)

            x_lo_of(0, 0, 0)
            x_lo_of(1, 0, 1)

            def add_row(g, half, par, s):
                t = S * g + s
                wait(pool, h_done, t + 1)
                if s % 2 == 0:
                    wait(pool, ld_row[s // 2], 16 * (g + 1))
                if s == 0:
                    wait(pool, st_x2[par], 16 * half)
                wait(pool, scattered[par * S + s], 16 * K2 * half)
                pool.tensor_tensor(x2_row[par][:, s, :], x_row[s // 2][:, s % 2, :], h[:, :], ALU.add).then_inc(x2_row_done, 1)

            def group_lo(g, par):
                for part_of, steps in enumerate((slice(0, S - 1), slice(S - 1, S))):
                    lo, src, hi = (ap.rearrange("p (k s b) -> p k s b", k=KC, s=S)[:, :, steps, :]
                                   for ap in (grp_lo, buf[par][:, :], grp_hi.bitcast(F32)))
                    wait(pool, grp_hi_done, 2 * g + 1 + part_of)
                    last = pool.tensor_tensor(lo, src, hi, ALU.subtract)
                last.then_inc(grp_lo_done, 1)

            def unit_lo(g, u):
                wait(pool, hi1_done, U * g + u + 1)
                pool.tensor_tensor(prod1_lo[u % 2][:, :], act_1, prod1_hi[u % 2][:, :].bitcast(F32), ALU.subtract).then_inc(lo1_done, 1)

            def scatter(par, s):
                for k in range(K2):
                    pool.indirect_dma_start(out=rows_x, out_offset=bass.IndirectOffsetOnAxis(ap=idx_x[par][:, s, k:k + 1], axis=0),
                                            in_=x2_row[par][:, s, :], in_offset=None).then_inc(scattered[par * S + s], 16)

            def scan_body(g, half, par):
                for s in range(S):
                    add_row(g, half, par, s)
                    if s < S - 2:
                        x_lo_of(S * g + s + 2, par, s + 2)
                    elif not (is_static(g) and g == G - 1):
                        x_lo_of(S * g + s + 2, 1 - par, s + 2 - S)
                    if s < S - 1 and not (is_static(g) and g < 2):
                        scatter(par, s + 1)
                    if s == S - 1:
                        if not (is_static(g) and g < 1):
                            wait(pool, idx_done, 3 * g)
                            pool.sem_inc(pool_go, 1)
                            scatter(1 - par, 0)
                        if not (is_static(g) and g == G - 1):
                            group_lo(g, par)
                    if not (is_static(g) and g == 0):
                        unit_lo(g - 1, s)

            groups(pool, scan_body)
            for s in range(1, S):
                scatter(0, s)
            pool.wait_ge(x2_row_done, T)
            pool.iota(tile_i, pattern=[[1, TILES]], base=0, channel_multiplier=0).then_inc(tile_i_done, 1)
            pool.wait_ge(idx_done, 3 * G)
            for s in range(S):
                scatter(1, s)

            pool.wait_ge(table_done, 1)
            n = 1
            pool.tensor_copy(y_at, place_all[:, :, :]).then_inc(y_idx_step, 1)
            for e in range(E_RT):
                pool.wait_ge(y_idx_step, n)
                pool.tensor_scalar(y_off, expert_all[:, :, :], float(e), y_base[:, e:e + 1], ALU.is_equal, ALU.mult)\
                    .then_inc(y_idx_step, 1)
                pool.wait_ge(y_idx_step, n + 1)
                pool.tensor_tensor(y_at, y_at, y_off, ALU.add).then_inc(y_idx_step, 1)
                n += 2
            pool.wait_ge(y_idx_step, n)
            pool.tensor_copy(idx_y, y_at).then_inc(y_idx_done, 1)
            for q in range(4):
                pool.wait_ge(st_t[q], 16 * TILES // 4)
            pool.wait_ge(y_idx_done, 1)

            def shared_body(g, half, par):
                wait(pool, gathered[par], 16 * S * K2 * half)
                cur = idx_y[:, g * S:(g + 1) * S, :] if is_static(g) else idx_y[:, bass.ds(g * S, S), :]
                pool.tensor_copy(idx_y_cur[par], cur).then_inc(idx_cur_done, 1)
                wait(pool, idx_cur_done, g + 1)
                wait(pool, out_done, g - 1)
                pool.sem_inc(pool_go, 1)
                for k, s in ((k, s) for k in range(K2) for s in range(S)):
                    pool.indirect_dma_start(out=got[par][k][:, s, :], out_offset=None, in_=rows_y,
                                            in_offset=bass.IndirectOffsetOnAxis(ap=idx_y_cur[par][:, s, k:k + 1], axis=0))\
                        .then_inc(gathered[par], 16)

            groups(pool, shared_body)


_INS = ["x", "xT", "condT", "cond", "wall", "biases", "wrT", "rbias"]


def _layout(i):
    import numpy as np
    a = {k: np.asarray(v) for k, v in i.items()}

    def tiles(w):
        return w.reshape(-1, P, w.shape[1]).transpose(1, 0, 2).reshape(P, -1)

    def shared(e):
        for f in range(F_SH // P):
            rows = slice(f * P, (f + 1) * P)
            yield from (tiles(a["L1_cond_s_w1"][e, rows].T), tiles(a["L1_cond_s_w3"][e, rows].T), a["L1_cond_s_w2"][e][:, rows].T)

    to_router = a["L1_cond_W_router"][:, :C].T
    parts = [tiles(a["L0_cond_w_W"]), *(tiles(np.concatenate([a[w], to_router], axis=1)) for w in ("L0_cond_wx_W", "L0_cond_wh_W")),
             *shared(0)]
    for e in range(E_RT):
        parts += [tiles(a["L1_cond_r_w1"][e].T), tiles(a["L1_cond_r_w2"][e].T)]
    parts += shared(1)
    wall = np.concatenate(parts, axis=1)
    return {
        "x": a["x"].reshape(B, T * C),
        "xT": a["x"].reshape(B, G, S, KC, P).transpose(1, 4, 3, 2, 0).reshape(G, P, KC * S * B),
        "condT": a["cond_1024"].reshape(B, KC, P).transpose(2, 1, 0).reshape(P, KC * B),
        "cond": a["cond_1024"],
        "wall": wall,
        "biases": np.concatenate([a["L0_cond_w_b"], a["L0_cond_wx_b"], a["L0_cond_wh_b"]]),
        "wrT": a["L1_cond_W_router"].reshape(E_RT, 2 * KC, P).transpose(2, 1, 0),
        "rbias": a["L1_cond_router_bias"],
    }


def kernel(**inputs):
    import numpy as _np
    import concourse.bacc as _bacc
    from concourse import mybir as _mybir
    from concourse.bass_utils import run_bass_kernel_spmd as _run

    nc = _bacc.Bacc("TRN2", target_bir_lowering=False, num_devices=1)
    laid = _layout(inputs)
    arrays, args = {}, []
    for name in _INS:
        a = _np.ascontiguousarray(laid[name])
        arrays[f"in_{name}"] = a
        args.append(nc.dram_tensor(f"in_{name}", a.shape, _mybir.dt.from_np(a.dtype), kind="ExternalInput").ap())
    args.append(nc.dram_tensor("out", (B, T * C), _mybir.dt.float32, kind="ExternalOutput").ap())
    build(nc, *args)
    r = _run(nc, [arrays], core_ids=[0])
    return r.results[0]["out"].reshape(B, T, C)
```
